# Optimizing a Trainium2 kernel written in Bass

```python
import numpy as np
import jax
import jax.numpy as jnp

def _softmax(x, axis=-1):
    return jax.nn.softmax(x, axis=axis)

def _gelu(x):
    return jax.nn.gelu(x, approximate=True)

def _silu(x):
    return jax.nn.silu(x)

def _sigmoid(x):
    return jax.nn.sigmoid(x)

def _layernorm(x, axis=-1, eps=1e-05):
    m = jnp.mean(x, axis=axis, keepdims=True)
    v = jnp.var(x, axis=axis, keepdims=True)
    return (x - m) / jnp.sqrt(v + eps)

def _scatter_add(tgt, idx, src, axis=0):
    return tgt.at[idx].add(src)

def _segment_sum(src, seg, n):
    return jax.ops.segment_sum(src, seg, n)
kernel_name = 'mk_xattn_ffn_d2_seqx_r8_c143a3'

def setup_inputs(seed: int=0):
    np.random.seed(seed)
    _w = jnp.asarray

    def _rec_inputs():
        import jax
        import jax.numpy as jnp
        _rk = jax.random.key(seed)
        x = 7.22e-05 + 1 * jax.random.normal(jax.random.fold_in(_rk, 1), (2, 256, 128), jnp.float32)
        _lenS = 256 - jax.random.randint(jax.random.fold_in(_rk, 7), (2,), 0, max(1, 256 // 4) + 1, jnp.int32)
        _lenS2 = 512 - jax.random.randint(jax.random.fold_in(_rk, 8), (2,), 0, max(1, 512 // 4) + 1, jnp.int32)
        _ctx_1024P = jax.random.normal(jax.random.fold_in(_rk, 11), (2, 16, 128), jnp.float32)
        _ctx_1024c = jax.random.dirichlet(jax.random.fold_in(_rk, 511), 0.3 * jnp.ones((16,), jnp.float32), (2, 512))
        _ctx_1024t = jnp.einsum('bsk,bkd->bsd', _ctx_1024c, _ctx_1024P)
        _ctx_1024t = _ctx_1024t * jax.lax.rsqrt(jnp.mean(jnp.square(_ctx_1024t)) + 1e-12) * 0.953939
        ctx_1024 = 4.13588e-05 + 0.999923 * (_ctx_1024t + 0.3 * jax.random.normal(jax.random.fold_in(_rk, 611), (2, 512, 128), jnp.float32))
        _validS = jnp.arange(256)[None, :] < _lenS[:, None]
        _validS2 = jnp.arange(512)[None, :] < _lenS2[:, None]
        _causal = jnp.tril(jnp.ones((256, 256), dtype=bool))
        mask_BxS2_bf1 = jnp.ones((2, 512), dtype=bool)
        return (x, ctx_1024, mask_BxS2_bf1)
    x, ctx_1024, mask_BxS2_bf1 = _rec_inputs()

    def _L0_xattn_setup():
        import jax, jax.numpy as jnp
        import numpy as np
        NEG_INF = -10000000000.0
        key = jax.random.key(seed)
        ks = jax.random.split(key, 8)
        B, S, D = (4, 256, 128)
        scale = 1.0 / np.sqrt(D)
        return {'query': jax.random.normal(ks[0], (B, S, D), jnp.float32), 'key': jax.random.normal(ks[1], (B, S, D), jnp.float32), 'value': jax.random.normal(ks[2], (B, S, D), jnp.float32), 'key_padding_mask': jnp.ones((B, S), dtype=bool), 'Wq': jax.random.normal(ks[3], (D, D), jnp.float32) * scale, 'Wk': jax.random.normal(ks[4], (D, D), jnp.float32) * scale, 'Wv': jax.random.normal(ks[5], (D, D), jnp.float32) * scale, 'Wo': jax.random.normal(ks[6], (D, D), jnp.float32) * scale, 'bo': jnp.zeros((D,), jnp.float32)}
    _L0_xattn_all = _L0_xattn_setup()
    _L0_xattn_in = {k: v for k, v in _L0_xattn_all.items() if k in ('Wq', 'Wk', 'Wv', 'Wo', 'bo')}
    del _L0_xattn_all

    def _L0_ffn_setup():
        import jax, jax.numpy as jnp
        import numpy as np
        N_EMBD = 128
        NUM_EXPERTS = 8
        TOP_K = 2
        D_FF = 4 * N_EMBD
        B, S = (4, 256)
        key = jax.random.key(seed)
        ks = jax.random.split(key, 7)
        scale = lambda fan_in: 1.0 / np.sqrt(fan_in)
        x = jax.random.normal(ks[0], (B, S, N_EMBD), dtype=jnp.float32)
        W_router = jax.random.normal(ks[1], (N_EMBD, NUM_EXPERTS), dtype=jnp.float32) * scale(N_EMBD)
        b_router = jnp.zeros((NUM_EXPERTS,), dtype=jnp.float32)
        W1 = jax.random.normal(ks[2], (NUM_EXPERTS, N_EMBD, D_FF), dtype=jnp.float32) * scale(N_EMBD)
        b1 = jnp.zeros((NUM_EXPERTS, D_FF), dtype=jnp.float32)
        W2 = jax.random.normal(ks[3], (NUM_EXPERTS, D_FF, N_EMBD), dtype=jnp.float32) * scale(D_FF)
        b2 = jnpp = jnp.zeros((NUM_EXPERTS, N_EMBD), dtype=jnp.float32)
        return {'x': x, 'W_router': W_router, 'b_router': b_router, 'W1': W1, 'b1': b1, 'W2': W2, 'b2': b2}
    _L0_ffn_all = _L0_ffn_setup()
    _L0_ffn_in = {k: v for k, v in _L0_ffn_all.items() if k in ('W_router', 'b_router', 'W1', 'b1', 'W2', 'b2')}
    del _L0_ffn_all

    def _L1_xattn_setup():
        import jax, jax.numpy as jnp
        import numpy as np
        DIM = 128
        HEADS = 16
        DHEAD = 64
        INNER = HEADS * DHEAD
        EPS = 1e-05

        def layer_norm(x, g, b):
            mu = jnp.mean(x, axis=-1, keepdims=True)
            var = jnp.mean(jnp.square(x - mu), axis=-1, keepdims=True)
            return (x - mu) * jax.lax.rsqrt(var + EPS) * g + b

        def apply_rope(x, cos, sin):
            d2 = x.shape[-1] // 2
            x1, x2 = (x[..., :d2], x[..., d2:])
            return jnp.concatenate([x1 * cos - x2 * sin, x2 * cos + x1 * sin], axis=-1)
        key = jax.random.key(seed)
        ks = jax.random.split(key, 10)
        B, N, S = (8, 32, 512)
        latents = jax.random.normal(ks[0], (B, N, DIM), dtype=jnp.float32)
        context = jax.random.normal(ks[1], (B, S, DIM), dtype=jnp.float32)
        cos = jax.random.uniform(ks[2], (S, DHEAD // 2), dtype=jnp.float32)
        sin = jax.random.uniform(ks[3], (S, DHEAD // 2), dtype=jnp.float32)
        init = lambda k, shp, fan_in: jax.random.normal(k, shp, dtype=jnp.float32) / np.sqrt(fan_in)
        return {'latents': latents, 'context': context, 'cos': cos, 'sin': sin, 'ln_lat_g': jnp.ones((DIM,), jnp.float32), 'ln_lat_b': jnp.zeros((DIM,), jnp.float32), 'ln_ctx_g': jnp.ones((DIM,), jnp.float32), 'ln_ctx_b': jnp.zeros((DIM,), jnp.float32), 'Wq': init(ks[4], (DIM, INNER), DIM), 'Wkv': init(ks[5], (DIM, 2 * INNER), DIM), 'Wo': init(ks[6], (INNER, DIM), INNER), 'bo': jnp.zeros((DIM,), jnp.float32)}
    _L1_xattn_all = _L1_xattn_setup()
    _L1_xattn_in = {k: v for k, v in _L1_xattn_all.items() if k in ('cos', 'sin', 'ln_lat_g', 'ln_lat_b', 'ln_ctx_g', 'ln_ctx_b', 'Wq', 'Wkv', 'Wo', 'bo')}
    del _L1_xattn_all

    def _L1_ffn_setup():
        import jax, jax.numpy as jnp
        import numpy as np
        IN_FEATURES = 128
        OUT_FEATURES = 128
        B, S = (8, 512)
        key = jax.random.key(seed)
        kx, kw = jax.random.split(key)
        x = jax.random.normal(kx, (B, S, IN_FEATURES), dtype=jnp.float32)
        weight = jax.random.normal(kw, (OUT_FEATURES, IN_FEATURES), dtype=jnp.float32) * 0.1
        bias = jnp.zeros((OUT_FEATURES,), dtype=jnp.float32)
        return {'x': x, 'weight': weight, 'bias': bias}
    _L1_ffn_all = _L1_ffn_setup()
    _L1_ffn_in = {k: v for k, v in _L1_ffn_all.items() if k in ('weight', 'bias')}
    del _L1_ffn_all
    return {'x': x, 'ctx_1024': ctx_1024, 'mask_BxS2_bf1': mask_BxS2_bf1, 'L0_xattn_Wq': _L0_xattn_in['Wq'], 'L0_xattn_Wk': _L0_xattn_in['Wk'], 'L0_xattn_Wv': _L0_xattn_in['Wv'], 'L0_xattn_Wo': _L0_xattn_in['Wo'], 'L0_xattn_bo': _L0_xattn_in['bo'], 'L0_ffn_W_router': _L0_ffn_in['W_router'], 'L0_ffn_b_router': _L0_ffn_in['b_router'], 'L0_ffn_W1': _L0_ffn_in['W1'], 'L0_ffn_b1': _L0_ffn_in['b1'], 'L0_ffn_W2': _L0_ffn_in['W2'], 'L0_ffn_b2': _L0_ffn_in['b2'], 'L1_xattn_cos': _L1_xattn_in['cos'], 'L1_xattn_sin': _L1_xattn_in['sin'], 'L1_xattn_ln_lat_g': _L1_xattn_in['ln_lat_g'], 'L1_xattn_ln_lat_b': _L1_xattn_in['ln_lat_b'], 'L1_xattn_ln_ctx_g': _L1_xattn_in['ln_ctx_g'], 'L1_xattn_ln_ctx_b': _L1_xattn_in['ln_ctx_b'], 'L1_xattn_Wq': _L1_xattn_in['Wq'], 'L1_xattn_Wkv': _L1_xattn_in['Wkv'], 'L1_xattn_Wo': _L1_xattn_in['Wo'], 'L1_xattn_bo': _L1_xattn_in['bo'], 'L1_ffn_weight': _L1_ffn_in['weight'], 'L1_ffn_bias': _L1_ffn_in['bias']}

def reference(x, ctx_1024, mask_BxS2_bf1, L0_xattn_Wq, L0_xattn_Wk, L0_xattn_Wv, L0_xattn_Wo, L0_xattn_bo, L0_ffn_W_router, L0_ffn_b_router, L0_ffn_W1, L0_ffn_b1, L0_ffn_W2, L0_ffn_b2, L1_xattn_cos, L1_xattn_sin, L1_xattn_ln_lat_g, L1_xattn_ln_lat_b, L1_xattn_ln_ctx_g, L1_xattn_ln_ctx_b, L1_xattn_Wq, L1_xattn_Wkv, L1_xattn_Wo, L1_xattn_bo, L1_ffn_weight, L1_ffn_bias):
    import jax
    import jax.numpy as jnp

    def _L0_xattn_ref(query, key, value, key_padding_mask, Wq, Wk, Wv, Wo, bo):
        import jax, jax.numpy as jnp
        import numpy as np
        NEG_INF = -10000000000.0
        nheads = 16
        B, Sq, D = query.shape
        d_k = D // nheads
        scale = 1.0 / jnp.sqrt(jnp.asarray(d_k, query.dtype))
        q = query @ Wq.T
        k = key @ Wk.T
        v = value @ Wv.T
        q = q.reshape(B, Sq, nheads, d_k)
        k = k.reshape(B, -1, nheads, d_k)
        v = v.reshape(B, -1, nheads, d_k)
        scores = jnp.einsum('bqhd,bkhd->bhqk', q, k) * scale
        mask = key_padding_mask[:, None, None, :]
        scores = jnp.where(mask, scores, jnp.asarray(NEG_INF, scores.dtype))
        attn = jax.nn.softmax(scores, axis=-1)
        out = jnp.einsum('bhqk,bkhd->bqhd', attn, v)
        out = out.reshape(B, Sq, D)
        return out @ Wo.T + bo

    def _L0_ffn_ref(x, W_router, b_router, W1, b1, W2, b2):
        import jax, jax.numpy as jnp
        import numpy as np
        N_EMBD = 128
        NUM_EXPERTS = 8
        TOP_K = 2
        D_FF = 4 * N_EMBD
        B, S = (4, 256)
        Bv, Sv, D = x.shape
        flat_x = x.reshape(-1, D)
        T = flat_x.shape[0]
        logits = flat_x @ W_router + b_router
        top_vals, top_idx = jax.lax.top_k(logits, TOP_K)
        neg_inf = jnp.full_like(logits, -jnp.inf)
        sparse_logits = neg_inf.at[jnp.arange(T)[:, None], top_idx].set(top_vals)
        router_weights = jax.nn.softmax(sparse_logits, axis=-1)
        final_output = jnp.zeros_like(flat_x)
        for e in range(NUM_EXPERTS):
            expert_mask = jnp.any(top_idx == e, axis=-1)
            h = jax.nn.relu(flat_x @ W1[e] + b1[e])
            y = h @ W2[e] + b2[e]
            w = router_weights[:, e] * expert_mask.astype(x.dtype)
            final_output = final_output + y * w[:, None]
        return final_output.reshape(Bv, Sv, D)

    def _L1_xattn_ref(latents, context, cos, sin, ln_lat_g, ln_lat_b, ln_ctx_g, ln_ctx_b, Wq, Wkv, Wo, bo):
        import jax, jax.numpy as jnp
        import numpy as np
        DIM = 128
        HEADS = 16
        DHEAD = 64
        INNER = HEADS * DHEAD
        EPS = 1e-05

        def layer_norm(x, g, b):
            mu = jnp.mean(x, axis=-1, keepdims=True)
            var = jnp.mean(jnp.square(x - mu), axis=-1, keepdims=True)
            return (x - mu) * jax.lax.rsqrt(var + EPS) * g + b

        def apply_rope(x, cos, sin):
            d2 = x.shape[-1] // 2
            x1, x2 = (x[..., :d2], x[..., d2:])
            return jnp.concatenate([x1 * cos - x2 * sin, x2 * cos + x1 * sin], axis=-1)
        b, n, _ = latents.shape
        s = context.shape[1]
        lat = layer_norm(latents, ln_lat_g, ln_lat_b)
        ctx = layer_norm(context, ln_ctx_g, ln_ctx_b)
        q = (lat @ Wq).reshape(b, n, HEADS, DHEAD).transpose(0, 2, 1, 3)
        kv = ctx @ Wkv
        k, v = jnp.split(kv, 2, axis=-1)
        k = k.reshape(b, s, HEADS, DHEAD).transpose(0, 2, 1, 3)
        v = v.reshape(b, s, HEADS, DHEAD).transpose(0, 2, 1, 3)
        k = apply_rope(k, cos[None, None], sin[None, None])
        scale = DHEAD ** (-0.5)
        attn = jnp.einsum('bhnd,bhsd->bhns', q, k) * scale
        attn = jnp.clip(attn, -11.0, 11.0)
        attn = jax.nn.softmax(attn, axis=-1)
        out = jnp.einsum('bhns,bhsd->bhnd', attn, v)
        out = out.transpose(0, 2, 1, 3).reshape(b, n, INNER)
        return out @ Wo + bo

    def _L1_ffn_ref(x, weight, bias):
        import jax, jax.numpy as jnp
        import numpy as np
        IN_FEATURES = 128
        OUT_FEATURES = 128
        B, S = (8, 512)
        w_scale = jnp.mean(jnp.abs(weight))
        q_weight = jnp.sign(weight) * (jnp.abs(weight) > 0.5 * w_scale).astype(weight.dtype)
        i_scale = jnp.max(jnp.abs(x)) / 127.0
        q_input = jnp.clip(jnp.round(x / i_scale), -128.0, 127.0)
        out = jnp.einsum('bsk,ok->bso', q_input, q_weight) * w_scale * i_scale
        out = out + bias
        return out
    x = x + _L0_xattn_ref(_layernorm(x, axis=-1), ctx_1024, ctx_1024, mask_BxS2_bf1, L0_xattn_Wq, L0_xattn_Wk, L0_xattn_Wv, L0_xattn_Wo, L0_xattn_bo)
    x = x + _L0_ffn_ref(_layernorm(x, axis=-1), L0_ffn_W_router, L0_ffn_b_router, L0_ffn_W1, L0_ffn_b1, L0_ffn_W2, L0_ffn_b2)
    x = x + _L1_xattn_ref(_layernorm(x, axis=-1), ctx_1024, L1_xattn_cos, L1_xattn_sin, L1_xattn_ln_lat_g, L1_xattn_ln_lat_b, L1_xattn_ln_ctx_g, L1_xattn_ln_ctx_b, L1_xattn_Wq, L1_xattn_Wkv, L1_xattn_Wo, L1_xattn_bo)
    x = x + _L1_ffn_ref(_layernorm(x, axis=-1), L1_ffn_weight, L1_ffn_bias)
    return x

_drawn_inputs = setup_inputs


def setup_inputs(seed=0):
    import zlib

    import numpy as np

    out = dict(_drawn_inputs(seed))
    spreads = {'L0_xattn_bo': (0.0, 0.1),
     'L0_ffn_b_router': (0.0, 0.1),
     'L0_ffn_b1': (0.0, 0.1),
     'L0_ffn_b2': (0.0, 0.1),
     'L1_xattn_ln_lat_g': (1.0, 0.6),
     'L1_xattn_ln_lat_b': (0.0, 0.71),
     'L1_xattn_ln_ctx_g': (1.0, 0.2),
     'L1_xattn_ln_ctx_b': (0.0, 0.1),
     'L1_xattn_bo': (0.0, 0.1),
     'L1_ffn_bias': (0.0, 0.1)}
    factors = {'L1_xattn_cos': 4.338, 'L1_xattn_sin': 4.128}
    for name, (base, spread) in spreads.items():
        noise = np.random.default_rng([zlib.crc32(name.encode()), seed]).standard_normal(out[name].shape)
        drawn = base * np.exp(spread * noise) if base else spread * noise
        out[name] = jnp.asarray(drawn.astype(out[name].dtype))
    for name, factor in factors.items():
        out[name] = (out[name] * factor).astype(out[name].dtype)
    return out
```

```python
import math
from contextlib import ExitStack

import numpy as np

import concourse.bass as bass
from concourse import mybir

P = 128
B, S, S2, D = 2, 256, 512, 128
T, C = B * S, B * S2
TT, CT = T // P, C // P
QT, KT = S // P, S2 // P
H = 16
DK0 = D // H
DK1 = 64
PAIRS = H // 2
G = H // 4
E, FF, FT = 8, 4 * D, 4
NPART = 3
ROWS = NPART * NPART * DK0
MASK_ROW = ROWS
MAX_ROW = 96
NEG = 1.0e10
EPS = 1e-5
CLIP = 11.0
RING = 8
UNITS = B * H
MAGIC = 1.5 * 2.0 ** 23


def build(nc, a, out):
    f32, bf16, u8 = mybir.dt.float32, mybir.dt.bfloat16, mybir.dt.uint8
    ALU, ACT, AX = mybir.AluOpType, mybir.ActivationFunctionType, mybir.AxisListType

    ctx = ExitStack()
    with ctx:
        def sb(name, shape, dt=f32):
            return ctx.enter_context(nc.sbuf_tensor(name, shape, dt))

        def sem(name):
            return ctx.enter_context(nc.semaphore(name))

        k_scr = nc.dram_tensor("k_scr", (B, NPART, P, S2), bf16, kind="Internal").ap()
        q_scr = nc.dram_tensor("q_scr", (B, NPART, P, S), bf16, kind="Internal").ap()
        m_scr = nc.dram_tensor("m_scr", (NPART, C), bf16, kind="Internal").ap()

        reg_k = sb("reg_k", [P, 8192])
        Ks = reg_k[:, :].bitcast(bf16).rearrange("p (h t) -> p h t", h=H)
        kT1 = reg_k[:, :].rearrange("p (a t) -> p a t", a=PAIRS)
        reg_q = sb("reg_q", [P, 4096])
        Qs = reg_q[:, :].bitcast(bf16).rearrange("p (h t) -> p h t", h=H)
        qT1 = reg_q[:, :].rearrange("p (a t) -> p a t", a=PAIRS)
        reg_p = sb("reg_p", [P, RING * 1024])
        prob = reg_p[:, :].rearrange("p (r n) -> p r n", r=RING)
        rot = reg_p[:, 0:4096].rearrange("p (r n) -> p r n", r=8)
        rkey = reg_p[:, 4096:6144].rearrange("p (r n) -> p r n", r=4)
        gt = reg_p[:, 6144:6400].rearrange("p (t e j) -> p t e j", t=TT, e=E)
        eq = reg_p[:, 6400:6656].rearrange("p (t e j) -> p t e j", t=TT, e=E)
        qz = reg_p[:, 0:512].rearrange("p (t d) -> p t d", t=TT)
        qzb = reg_p[:, 512:768].bitcast(bf16).rearrange("p (t d) -> p t d", t=TT)
        qzT = reg_p[:, 768:1024].bitcast(bf16)
        reg_z = sb("reg_z", [P, 4096])
        kf = reg_z[:, 0:1024]
        qf = reg_z[:, 1024:1536]
        res = reg_z[:, 1536:2048]
        kparts = reg_z[:, 2048:2048 + 768].bitcast(bf16).rearrange("p (j t) -> p j t", j=NPART)
        qparts = reg_z[:, 2816:2816 + 384].bitcast(bf16).rearrange("p (j t) -> p j t", j=NPART)
        kparts1 = reg_z[:, 3200:3200 + 768].bitcast(bf16).rearrange("p (j t) -> p j t", j=NPART)
        reg_y = sb("reg_y", [P, 384])
        qparts1 = reg_y[:, :].bitcast(bf16).rearrange("p (j t) -> p j t", j=NPART)
        o0 = reg_z[:, 0:2048].rearrange("p (g q) -> p g q", g=B * G)
        on0 = reg_z[:, 2048:2560].rearrange("p (t h d) -> p t h d", t=TT, h=H)
        oT0 = reg_z[:, 2560:3072]
        hT = reg_z[:, :].rearrange("p (r f t) -> p r f t", r=2, f=FT)
        oT1 = reg_z[:, :].rearrange("p (a t) -> p a t", a=PAIRS)
        w1 = sb("w1", [P, E, FF])
        w2 = sb("w2", [P, E, FT, D])
        wv1 = reg_p[:, 7168:8192]
        wo1 = w1[:, 0:2, :].rearrange("p e (a d) -> p (e a) d", a=PAIRS // 2)
        v1 = sb("v1", [P, CT, H * DK1])
        v0 = sb("v0", [P, CT, H, DK0 + 1])
        ctx_tok = sb("ctx_tok", [P, CT, D])
        wq1 = ctx_tok[:, :, :].rearrange("p c d -> p (c d)")
        ctxT = sb("ctxT", [P, C])
        x = sb("x", [P, TT, D])
        xb = sb("xb", [P, TT, D])
        y = sb("y", [P, TT, D])
        yT = sb("yT", [P, T])
        l0w = sb("l0w", [P, 4, D])
        wk1 = sb("wk1", [P, 2 * G, P])
        cosT = sb("cosT", [P, S2])
        sinT = sb("sinT", [P, S2])
        maskb = sb("maskb", [P, C], u8)
        mask16 = sb("mask16", [16, C // 16], u8)
        mval = sb("mval", [16, 2, C // 16])
        mpart = sb("mpart", [16, NPART, C // 16], bf16)
        bias0, bias1, bias2 = (sb(n, [P, D]) for n in ("bias0", "bias1", "bias2"))
        lncol = sb("lncol", [P, 4])
        wr = sb("wr", [P, E])
        brow = sb("brow", [P, E])
        b1 = sb("b1", [P, E, FT])
        b2 = sb("b2", [E, D])
        wf = sb("wf", [P, D])
        ident = sb("ident", [P, P])
        identb = sb("identb", [P, P], bf16)
        ones = sb("ones", [P, P])
        tri = sb("tri", [P, E, E])
        mhalf = sb("mhalf", [P, 1])
        st = sb("st", [P, CT, 6])
        mv = sb("mv", [P, CT, 2])
        ve = sb("ve", [P, CT])
        rstd = sb("rstd", [P, CT])
        nmax = sb("nmax", [P, B, QT, H])
        maxres = sb("maxres", [QT * H, P])
        maxpart = sb("maxpart", [QT * H, B, NPART, P], bf16)
        rs0 = sb("rs0", [P, TT, H])
        rs1 = sb("rs1", [P, 2, S])
        lg = sb("lg", [P, TT, E])
        rank = sb("rank", [P, TT, E])
        top = sb("top", [P, TT])
        ex = sb("ex", [P, TT, E])
        wgt = sb("wgt", [P, TT, E])
        wT = sb("wT", [E, T])
        qw = sb("qw", [P, 2, D], bf16)
        sc = sb("sc", [P, 8])

        st2 = [ctx.enter_context(nc.psum_tensor(f"st{i}", [P, 1024], f32)) for i in range(2)]
        b4, b5, b6, b7 = (ctx.enter_context(nc.psum_tensor(f"b{i}", [P, 512], f32)) for i in (4, 5, 6, 7))
        bank = [st2[0][:, 0:512], st2[0][:, 512:1024], st2[1][:, 0:512], st2[1][:, 512:1024],
                b4[:, :], b5[:, :], b6[:, :], b7[:, :]]

        in_x, in_w0, in_ctxT, in_mask, in_ctx, in_cols, in_wv, in_rope, in_wk, in_small, in_w1, in_w2, \
            in_wq, in_wo, in_wf = (sem("in_" + n) for n in (
                "x", "w0", "ctxT", "mask", "ctx", "cols", "wv", "rope", "wk", "small", "w1", "w2", "wq", "wo", "wf"))
        consts = sem("consts")
        pool_step = sem("pool_step")
        stats = sem("stats")
        pow_done = sem("pow_done")
        dve_step = sem("dve_step")
        normed = sem("normed")
        tr = sem("tr")
        k0_ps, q0_ps, v0_ps = sem("k0_ps"), sem("q0_ps"), sem("v0_ps")
        q0_f, v0_sb = sem("q0_f"), sem("v0_sb")
        parts = sem("parts")
        mparts = sem("mparts")
        scr = [sem(f"scr{b}") for b in range(B)]
        scr_m = sem("scr_m")
        stack = [sem(f"stack{b}") for b in range(B)]
        stack_m = sem("stack_m")
        ctxn = sem("ctxn")
        v1_ps, v1_sb = sem("v1_ps"), sem("v1_sb")
        mx_ps, mx_done = sem("mx_ps"), sem("mx_done")
        mt_ps, mt_parts = sem("mt_ps"), sem("mt_parts")
        max_rows = [sem(f"max_rows{b}") for b in range(B)]
        st_ps, st_exp = sem("st_ps"), sem("st_exp")
        clipped = sem("clipped")
        pv0, o0_sb = sem("pv0"), sem("o0_sb")
        t1_ps, on_sb, t2_ps, oT_sb, wo0_ps = (sem(n) for n in ("t1_ps", "on_sb", "t2_ps", "oT_sb", "wo0_ps"))
        yT_sb = sem("yT_sb")
        rt_ps, rt_lg, rt_ex, rt_w, rt_wps, rt_wT, rt_b2 = (sem("rt_" + n) for n in ("ps", "lg", "ex", "w", "wps", "wT", "b2"))
        h_ps, h_sb, y_ps, y_acc = sem("h_ps"), sem("h_sb"), sem("y_ps"), sem("y_acc")
        kp_ps, rot_m, rkey_sb = sem("kp_ps"), sem("rot_m"), sem("rkey_sb")
        rkey_out = [sem(f"rkey_out{i}") for i in range(2)]
        b2_sb = sem("b2_sb")
        xbias = sem("xbias")
        q1_ps, q1_sb = sem("q1_ps"), sem("q1_sb")
        pv1, o1_sb, wo1_ps = sem("pv1"), sem("o1_sb"), sem("wo1_ps")
        sc_ps, sc_sb = sem("sc_ps"), sem("sc_sb")
        qz_sb, qz_ps, qzT_sb, f_ps, fin = (sem(n) for n in ("qz_sb", "qz_ps", "qzT_sb", "f_ps", "fin"))
        stored = sem("stored")

        block = ctx.enter_context(nc.Block())

        order0 = [("mx", 0, h, t) for h in range(H) for t in range(QT)] + [("mt", 0)]
        mx1 = [("mx", 1, h, t) for h in range(H) for t in range(QT)]
        order0 += mx1[:6]
        rest = mx1[6:]
        for h in range(H):
            order0.append(("st", h))
            order0 += rest[:2]
            rest = rest[2:]
            if h % 4 == 1 and h > 4:
                order0.append(("pv", h // 4 - 1))
        order0.append(("mt", 1))
        order0.append(("pv", 3))
        for h in range(H):
            order0.append(("st", H + h))
            if h % 4 == 1 and h > 4:
                order0.append(("pv", G + h // 4 - 1))
        order0.append(("pv", 2 * G - 1))

        @block.sync
        def _(sp):
            def load(dst, src, s):
                sp.dma_start(dst, src).then_inc(s, 16)

            load(x[:, :, :], a["x"].rearrange("t p d -> p t d"), in_x)
            load(ctxT[:, :], a["ctxT"], in_ctxT)
            load(l0w[:, :, :], a["l0w"].rearrange("n p d -> p n d"), in_w0)
            load(maskb[:, :], a["mask"].broadcast_to([P, C]), in_mask)
            load(mask16[:, :], a["mask"].rearrange("a (p n) -> (a p) n", p=16), in_mask)
            load(ctx_tok[:, :, :], a["ctx"].rearrange("t p d -> p t d"), in_ctx)
            load(wv1, a["wv1"], in_wv)
            sp.wait_ge(mparts, 1)
            sp.dma_start(m_scr.rearrange("j (p n) -> p j n", p=16), mpart[:, :, :]).then_inc(scr_m, 16)
            for b in range(B):
                kp = kparts if b == 0 else kparts1
                qp = qparts if b == 0 else qparts1
                sp.wait_ge(parts, b + 1)
                sp.dma_start(k_scr[b].rearrange("j p t -> p j t"), kp).then_inc(scr[b], 16)
                sp.dma_start(q_scr[b].rearrange("j p t -> p j t"), qp).then_inc(scr[b], 16)
                if b == 0:
                    sp.wait_ge(consts, 2)
                sp.wait_ge(scr[b], 32)
                for i in range(NPART):
                    r = i * NPART * DK0
                    sp.dma_start(Ks[r:r + NPART * DK0, :, b * S2:(b + 1) * S2],
                                 k_scr[b].rearrange("j (d h) t -> (j d) h t", h=H)).then_inc(stack[b], 16)
                    for j in range(NPART):
                        sp.dma_start(Qs[r + j * DK0:r + (j + 1) * DK0, :, b * S:(b + 1) * S],
                                     q_scr[b, i].rearrange("(d h) t -> d h t", h=H)).then_inc(stack[b], 16)
                if b == 0:
                    sp.wait_ge(scr_m, 16)
                    for j in range(NPART):
                        sp.dma_start(Ks[MASK_ROW + j:MASK_ROW + j + 1, :, :],
                                     m_scr[j:j + 1, :].rearrange("j (o t) -> j o t", o=1).broadcast_to([1, H, C])
                                     ).then_inc(stack_m, 16)
            for b in range(B):
                sp.wait_ge(mt_parts, b + 1)
                for t in range(QT):
                    for j in range(NPART):
                        sp.dma_start(Qs[MAX_ROW + j:MAX_ROW + j + 1, :, b * S + t * P:b * S + (t + 1) * P],
                                     maxpart[t * H:(t + 1) * H, b, j, :]).then_inc(max_rows[b], 16)
            sp.wait_ge(tr, 3)
            sp.dma_start(wq1, a["wq1"]).then_inc(in_wq, 16)
            sp.wait_ge(st_ps, UNITS)
            for n in range(B * G):
                g, b = n // B, n % B
                sp.wait_ge(rkey_sb, 2 * (n + 1))
                for part in range(2):
                    for j in range(4):
                        head = 4 * g + j
                        r = 64 * (head % 2) + 32 * part
                        sp.dma_start(kT1[r:r + 32, head // 2, b * S2:(b + 1) * S2],
                                     rkey[32 * j:32 * j + 32, 2 * (n % 2) + part, :]).then_inc(rkey_out[n % 2], 16)
            sp.wait_ge(h_ps, E * FT)
            sp.dma_start(wo1, a["wo1"].rearrange("(a p) d -> p a d", p=P)).then_inc(in_wo, 16)
            sp.wait_ge(fin, 1)
            sp.dma_start(out.rearrange("t p d -> p t d"), qz[:, :, :]).then_inc(stored, 16)
            sp.wait_ge(stored, 16)

        @block.gpsimd
        def _(pool):
            steps = [0]

            def link(ins):
                steps[0] += 1
                ins.then_inc(pool_step, 1)
                pool.wait_ge(pool_step, steps[0])

            nc.gpsimd.memset(mhalf[:, :], -0.5)
            nc.gpsimd.memset(ones[:, :], 1.0)
            nc.gpsimd.memset(tri[:, :, :], 1.0)
            link(nc.gpsimd.memset(ident[:, :], 0.0))
            link(nc.gpsimd.affine_select(out=ident[:, :], in_=ident[:, :], compare_op=ALU.not_equal, fill=1.0,
                                         base=0, pattern=[[-1, P]], channel_multiplier=1))
            link(nc.gpsimd.tensor_copy(identb[:, :], ident[:, :]))
            nc.gpsimd.affine_select(out=tri[:, :, :], in_=tri[:, :, :], compare_op=ALU.is_ge, fill=0.0,
                                    base=-1, pattern=[[1, E], [-1, E]], channel_multiplier=0).then_inc(consts, 1)

            def power(n, tiles):
                pool.wait_ge(stats, n)
                nc.gpsimd.tensor_tensor(rstd[:, 0:tiles], ve[:, 0:tiles], mhalf[:, :].broadcast_to([P, tiles]),
                                        ALU.pow).then_inc(pow_done, 1)

            power(1, TT)
            pool.wait_ge(pow_done, 1)
            link(nc.gpsimd.memset(reg_q[64:96, :].bitcast(bf16), 1.0))
            link(nc.gpsimd.memset(reg_q[96:128, :], 0.0))
            link(nc.gpsimd.memset(reg_k[64:96, :], 0.0))
            link(nc.gpsimd.memset(reg_k[96:128, :].bitcast(bf16), 1.0))
            nc.gpsimd.memset(v0[:, :, :, DK0:DK0 + 1], 1.0).then_inc(consts, 1)
            power(2, CT)
            pool.wait_ge(in_small, 16 * 8)
            pool.wait_ge(normed, 1)
            nc.gpsimd.tensor_tensor(xb[:, :, :], x[:, :, :], bias0[:, None, :].broadcast_to([P, TT, D]),
                                    ALU.add).then_inc(xbias, 1)
            power(3, TT)
            for n in range(B * G):
                pool.wait_ge(rot_m, n + 1)
                if n >= 2:
                    pool.wait_ge(rkey_out[n % 2], 16 * 8 * (n // 2))
                q4 = 4 * (n % 2)
                nc.gpsimd.tensor_tensor(rkey[:, 2 * (n % 2), :], rot[:, q4, :], rot[:, q4 + 1, :],
                                        ALU.subtract).then_inc(rkey_sb, 1)
                nc.gpsimd.tensor_tensor(rkey[:, 2 * (n % 2) + 1, :], rot[:, q4 + 2, :], rot[:, q4 + 3, :],
                                        ALU.add).then_inc(rkey_sb, 1)
            power(4, TT)
            nc.gpsimd.tensor_tensor(xb[:, :, :], x[:, :, :], bias1[:, None, :].broadcast_to([P, TT, D]),
                                    ALU.add).then_inc(xbias, 1)
            power(5, TT)
            power(6, TT)
            nc.gpsimd.tensor_tensor(xb[:, :, :], x[:, :, :], bias2[:, None, :].broadcast_to([P, TT, D]),
                                    ALU.add).then_inc(xbias, 1)

        @block.scalar
        def _(act):
            def load(dst, src, s):
                act.dma_start(dst, src).then_inc(s, 16)

            load(lncol[:, :], a["lncol"], in_cols)
            for dst, name in ((bias0, "bias0"), (bias1, "bias1"), (bias2, "bias2"), (brow, "brow")):
                load(dst[:, :], a[name].broadcast_to([P, dst.shape[1]]), in_small)
            load(wr[:, :], a["wr"], in_small)
            load(b1[:, :, :], a["b1"], in_small)
            load(b2[:, :], a["b2"], in_small)
            load(wf[:, :], a["wf"], in_small)
            for q in range(4):
                load(cosT[32 * q:32 * q + 32, :], a["cosT"], in_rope)
                load(sinT[32 * q:32 * q + 32, :], a["sinT"], in_rope)
            load(wk1[:, :, :], a["wk1"].rearrange("p (n c) -> p n c", n=2 * G), in_wk)
            load(w1[:, :, :], a["w1"].rearrange("e p f -> p e f"), in_w1)
            load(w2[:, :, :, :], a["w2"].rearrange("e (f p) d -> p e f d", p=P), in_w2)
            act.wait_ge(q0_ps, 1)
            nc.scalar.activation(qf, bank[6], ACT.Copy, scale=1.0 / math.sqrt(DK0)).then_inc(q0_f, 1)
            for i in range(2):
                act.wait_ge(v0_ps, i + 1)
                nc.scalar.activation(v0[:, 4 * i:4 * i + 4, :, 0:DK0],
                                     bank[2 + i].rearrange("p (c h d) -> p c h d", c=4, h=H),
                                     ACT.Copy).then_inc(v0_sb, 1)
            act.wait_ge(in_cols, 16)
            for i in range(2):
                act.wait_ge(tr, 2 + i)
                nc.scalar.activation(ctxT[:, 512 * i:512 * i + 512], bank[i], ACT.Identity,
                                     scale=lncol[:, 2:3], bias=lncol[:, 3:4]).then_inc(ctxn, 1)
            for n in range(2 * CT):
                act.wait_ge(v1_ps, n + 1)
                nc.scalar.activation(v1[:, n // 2, 512 * (n % 2):512 * (n % 2) + 512], bank[n % 4],
                                     ACT.Copy).then_inc(v1_sb, 1)
            for u in range(UNITS):
                act.wait_ge(st_ps, u + 1)
                if u >= RING:
                    act.wait_ge(pv0, u // 4 - 1)
                nc.scalar.activation(prob[:, u % RING, :], st2[u % 2][:, :], ACT.Exp).then_inc(st_exp, 1)
            act.wait_ge(tr, 4)
            nc.scalar.activation(yT[:, :], bank[7], ACT.Copy).then_inc(yT_sb, 1)
            act.wait_ge(rt_lg, 1)
            nc.scalar.activation(ex[:, :, :], lg[:, :, :], ACT.Exp).then_inc(rt_ex, 1)
            for n in range(E * FT):
                e, f = n // FT, n % FT
                act.wait_ge(h_ps, n + 1)
                if e >= 2:
                    act.wait_ge(y_ps, e - 1)
                nc.scalar.activation(hT[:, e % 2, f, :], bank[n % 4], ACT.Relu,
                                     bias=b1[:, e, f:f + 1]).then_inc(h_sb, 1)
            act.wait_ge(tr, 5)
            nc.scalar.activation(yT[:, :], bank[7], ACT.Identity, scale=lncol[:, 0:1],
                                 bias=lncol[:, 1:2]).then_inc(yT_sb, 1)
            for p in range(PAIRS):
                act.wait_ge(q1_ps, p + 1)
                nc.scalar.activation(qT1[:, p, :], bank[4 + p % 2], ACT.Copy).then_inc(q1_sb, 1)
            for u in range(UNITS):
                act.wait_ge(st_ps, UNITS + u + 1)
                if u >= RING:
                    act.wait_ge(pv1, u // 2 - 3)
                nc.scalar.activation(prob[:, u % RING, :], st2[u % 2][:, :], ACT.Exp,
                                     scale=DK1 ** -0.5).then_inc(st_exp, 1)

        @block.vector
        def _(dve):
            steps = [0]

            def link(ins):
                steps[0] += 1
                ins.then_inc(dve_step, 1)
                dve.wait_ge(dve_step, steps[0])

            norms = [0]

            def layer_norm(dst, src, tiles):
                norms[0] += 1
                for t in range(tiles):
                    last = nc.vector.bn_stats(st[:, t, :], src[:, t, :])
                link(last)
                for t in range(tiles):
                    last = nc.vector.bn_aggr(mv[:, t, :], st[:, t, :])
                link(last)
                nc.vector.tensor_scalar_add(ve[:, 0:tiles], mv[:, 0:tiles, 1], EPS).then_inc(stats, 1)
                dve.wait_ge(pow_done, norms[0])
                for t in range(tiles):
                    last = nc.vector.tensor_scalar(dst[:, t, :], src[:, t, :], mv[:, t, 0:1], rstd[:, t:t + 1],
                                                   ALU.subtract, ALU.mult)
                last.then_inc(normed, 1)
                return norms[0]

            def split(dst, src, tmp):
                link(nc.vector.tensor_copy(dst[0], src))
                link(nc.vector.tensor_tensor(tmp, src, dst[0], ALU.subtract))
                link(nc.vector.tensor_copy(dst[1], tmp))
                return nc.vector.tensor_tensor(dst[2], tmp, dst[1], ALU.subtract)

            dve.wait_ge(in_x, 16)
            layer_norm(y, x, TT)
            dve.wait_ge(in_mask, 32)
            link(nc.vector.tensor_scalar(mval[:, 0, :], mask16[:, :], NEG, NEG, ALU.mult, ALU.subtract))
            split([mpart[:, j, :] for j in range(NPART)], mval[:, 0, :], mval[:, 1, :]).then_inc(mparts, 1)
            for b in range(B):
                dve.wait_ge(k0_ps, b + 1)
                last = nc.vector.tensor_tensor(kf[:, b * S2:(b + 1) * S2], bank[4 + b],
                                               maskb[:, b * S2:(b + 1) * S2], ALU.mult)
            link(last)
            dve.wait_ge(tr, 1)
            nc.vector.tensor_copy(yT[:, :], bank[7]).then_inc(yT_sb, 1)
            for b in range(B):
                kp = kparts if b == 0 else kparts1
                qp = qparts if b == 0 else qparts1
                split([kp[:, j, :] for j in range(NPART)], kf[:, b * S2:(b + 1) * S2], res)
                if b == 0:
                    dve.wait_ge(q0_f, 1)
                    nc.vector.memset(bank[6], 0.0)
                link(nc.vector.tensor_copy(qp[:, 0, :], qf[:, b * S:(b + 1) * S]))
                split([qp[:, j, :] for j in range(NPART)], qf[:, b * S:(b + 1) * S], res[:, 0:S]).then_inc(parts, 1)
            dve.wait_ge(in_ctx, 16)
            layer_norm(ctx_tok, ctx_tok, CT)

            mx = 0
            for item in order0:
                if item[0] == "mx":
                    _, b, h, t = item
                    mx += 1
                    dve.wait_ge(mx_ps, mx)
                    nc.vector.tensor_reduce(nmax[:, b, t, h:h + 1], bank[4 + mx % 2], AX.X, ALU.max,
                                            negate=True).then_inc(mx_done, 1)
                elif item[0] == "mt":
                    b = item[1]
                    dve.wait_ge(mt_ps, b + 1)
                    split([maxpart[:, b, j, :] for j in range(NPART)], bank[7][0:QT * H, 0:P],
                          maxres[:, :]).then_inc(mt_parts, 1)
                elif item[0] == "pv":
                    g = item[1]
                    dve.wait_ge(pv0, g + 1)
                    if g == 0:
                        dve.wait_ge(stack[1], 16 * 12)
                    nc.vector.tensor_copy(o0[:, g, :], bank[6][:, 0:S]).then_inc(o0_sb, 1)

            for t in range(TT):
                dve.wait_ge(t1_ps, t + 1)
                o = bank[t].rearrange("p (h c) -> p h c", h=H)
                link(nc.vector.reciprocal(rs0[:, t, :], o[:, :, DK0]))
                nc.vector.tensor_tensor(on0[:, t, :, :], o[:, :, 0:DK0],
                                        rs0[:, t, :, None].broadcast_to([P, H, DK0]), ALU.mult).then_inc(on_sb, 1)
            dve.wait_ge(t2_ps, 1)
            nc.vector.tensor_copy(oT0[:, :], bank[7]).then_inc(oT_sb, 1)
            dve.wait_ge(xbias, 1)
            dve.wait_ge(wo0_ps, 1)
            link(nc.vector.tensor_tensor(x[:, :, :], bank[6].rearrange("p (t d) -> p t d", t=TT), xb[:, :, :], ALU.add))
            layer_norm(y, x, TT)

            dve.wait_ge(in_small, 16 * 8)
            dve.wait_ge(consts, 1)
            dve.wait_ge(rt_ps, 1)
            link(nc.vector.tensor_tensor(lg[:, :, :], bank[6][:, 0:TT * E].rearrange("p (t e) -> p t e", t=TT),
                                         brow[:, None, :].broadcast_to([P, TT, E]), ALU.add))
            link(nc.vector.tensor_reduce(top[:, :], lg[:, :, :], AX.X, ALU.max))
            for t in range(TT):
                lj = lg[:, t, None, :].broadcast_to([P, E, E])
                le = lg[:, t, :, None].broadcast_to([P, E, E])
                nc.vector.tensor_tensor(gt[:, t, :, :], lj, le, ALU.is_gt)
                last = nc.vector.tensor_tensor(eq[:, t, :, :], lj, le, ALU.is_equal)
            link(last)
            nc.vector.tensor_tensor(lg[:, :, :], lg[:, :, :], top[:, :, None].broadcast_to([P, TT, E]),
                                    ALU.subtract).then_inc(rt_lg, 1)
            link(nc.vector.tensor_tensor(eq[:, :, :, :], eq[:, :, :, :], tri[:, None, :, :].broadcast_to([P, TT, E, E]), ALU.mult))
            link(nc.vector.tensor_tensor(gt[:, :, :, :], gt[:, :, :, :], eq[:, :, :, :], ALU.add))
            link(nc.vector.tensor_reduce(rank[:, :, :], gt[:, :, :, :], AX.X, ALU.add))
            dve.wait_ge(rt_ex, 1)
            link(nc.vector.scalar_tensor_tensor(out=wgt[:, :, :], in0=rank[:, :, :], scalar=2.0, in1=ex[:, :, :],
                                                op0=ALU.is_lt, op1=ALU.mult))
            link(nc.vector.tensor_reduce(top[:, :], wgt[:, :, :], AX.X, ALU.add))
            link(nc.vector.reciprocal(top[:, :], top[:, :]))
            nc.vector.tensor_tensor(wgt[:, :, :], wgt[:, :, :], top[:, :, None].broadcast_to([P, TT, E]),
                                    ALU.mult).then_inc(rt_w, 1)
            dve.wait_ge(rt_wps, 1)
            nc.vector.tensor_copy(wT[:, :], bank[7][0:E, :]).then_inc(rt_wT, 1)
            dve.wait_ge(rt_b2, 1)
            nc.vector.tensor_tensor(x[:, :, :], bank[4].rearrange("p (t d) -> p t d", t=TT), x[:, :, :],
                                    ALU.add).then_inc(b2_sb, 1)
            dve.wait_ge(b2_sb, 1)

            dve.wait_ge(in_rope, 16 * 8)
            for e in range(E):
                dve.wait_ge(kp_ps, e + 1)
                if e >= 2:
                    dve.wait_ge(rkey_sb, 2 * (e - 1))
                q4 = 4 * (e % 2)
                nc.vector.tensor_tensor(rot[:, q4, :], bank[6], cosT[:, :], ALU.mult)
                nc.vector.tensor_tensor(rot[:, q4 + 1, :], bank[7], sinT[:, :], ALU.mult)
                nc.vector.tensor_tensor(rot[:, q4 + 2, :], bank[7], cosT[:, :], ALU.mult)
                nc.vector.tensor_tensor(rot[:, q4 + 3, :], bank[6], sinT[:, :], ALU.mult).then_inc(rot_m, 1)
                dve.wait_ge(y_ps, e + 1)
                for t in range(TT):
                    last = nc.vector.scalar_tensor_tensor(
                        out=x[:, t, :], in0=bank[4 + e % 2][:, t * D:(t + 1) * D], scalar=wgt[:, t, e:e + 1],
                        in1=x[:, t, :], op0=ALU.mult, op1=ALU.add)
                last.then_inc(y_acc, 1)
                dve.wait_ge(y_acc, e + 1)

            layer_norm(y, x, TT)
            dve.wait_ge(normed, 4)
            layer_norm(y, y, TT)

            for u in range(UNITS):
                dve.wait_ge(st_exp, UNITS + u + 1)
                nc.vector.tensor_scalar(prob[:, u % RING, :], prob[:, u % RING, :], math.exp(-CLIP), math.exp(CLIP),
                                        ALU.max, ALU.min).then_inc(clipped, 1)
                if u % 2 == 1 and u >= 3:
                    n = u // 2 - 1
                    dve.wait_ge(pv1, n + 1)
                    link(nc.vector.reciprocal(rs1[:, n % 2, :], bank[4 + n % 2][:, S:2 * S]))
                    nc.vector.tensor_tensor(oT1[:, n % PAIRS, (n // PAIRS) * S:(n // PAIRS + 1) * S],
                                            bank[4 + n % 2][:, 0:S], rs1[:, n % 2, :], ALU.mult).then_inc(o1_sb, 1)
            n = UNITS // 2 - 1
            dve.wait_ge(pv1, n + 1)
            link(nc.vector.reciprocal(rs1[:, n % 2, :], bank[4 + n % 2][:, S:2 * S]))
            nc.vector.tensor_tensor(oT1[:, n % PAIRS, (n // PAIRS) * S:(n // PAIRS + 1) * S],
                                    bank[4 + n % 2][:, 0:S], rs1[:, n % 2, :], ALU.mult).then_inc(o1_sb, 1)

            link(nc.vector.tensor_reduce(sc[:, 0:1], wf[:, :], AX.X, ALU.add, apply_absolute_value=True))
            nc.vector.tensor_copy(sc[:, 1:2], sc[:, 0:1]).then_inc(sc_sb, 1)
            dve.wait_ge(sc_ps, 1)
            link(nc.vector.tensor_scalar_mul(sc[:, 2:3], bank[7][:, 0:1], 1.0 / (D * D)))
            link(nc.vector.tensor_scalar_mul(sc[:, 3:4], sc[:, 2:3], -0.5))
            link(nc.vector.tensor_scalar(qw[:, 1, :], wf[:, :], sc[:, 3:4], None, ALU.is_lt))
            link(nc.vector.tensor_scalar_mul(sc[:, 4:5], sc[:, 2:3], 0.5))
            link(nc.vector.scalar_tensor_tensor(out=qw[:, 0, :], in0=wf[:, :], scalar=sc[:, 4:5], in1=qw[:, 1, :],
                                                op0=ALU.is_gt, op1=ALU.subtract))

            dve.wait_ge(xbias, 2)
            dve.wait_ge(wo1_ps, TT)
            link(nc.vector.tensor_tensor(x[:, :, :], bank[6].rearrange("p (t d) -> p t d", t=TT), xb[:, :, :], ALU.add))
            layer_norm(y, x, TT)
            dve.wait_ge(normed, 6)
            nc.vector.tensor_reduce(sc[:, 0:1], y[:, :, :], AX.XY, ALU.max, apply_absolute_value=True).then_inc(sc_sb, 1)
            dve.wait_ge(sc_ps, 2)
            nc.vector.tensor_reduce(sc[0:1, 1:2], bank[7][0:1, 0:P], AX.X, ALU.max).then_inc(sc_sb, 1)
            dve.wait_ge(sc_ps, 3)
            link(nc.vector.tensor_scalar_mul(sc[:, 5:6], bank[7][:, 0:1], 1.0 / 127.0))
            link(nc.vector.reciprocal(sc[:, 6:7], sc[:, 5:6]))
            link(nc.vector.tensor_tensor(sc[:, 7:8], sc[:, 5:6], sc[:, 2:3], ALU.mult))
            link(nc.vector.tensor_scalar_mul(qz[:, :, :], y[:, :, :], sc[:, 6:7]))
            link(nc.vector.tensor_scalar(qz[:, :, :], qz[:, :, :], MAGIC, MAGIC, ALU.add, ALU.subtract))
            nc.vector.tensor_scalar(qzb[:, :, :], qz[:, :, :], -128.0, 127.0, ALU.max, ALU.min).then_inc(qz_sb, 1)
            dve.wait_ge(qz_ps, 1)
            nc.vector.tensor_copy(qzT[:, :], bank[4].bitcast(bf16)[:, 0:T]).then_inc(qzT_sb, 1)
            dve.wait_ge(xbias, 3)
            dve.wait_ge(f_ps, 1)
            nc.vector.scalar_tensor_tensor(out=qz[:, :, :], in0=bank[6].rearrange("p (t d) -> p t d", t=TT),
                                           scalar=sc[:, 7:8], in1=xb[:, :, :], op0=ALU.mult, op1=ALU.add).then_inc(fin, 1)

        @block.tensor
        def _(pe):
            def mm(o, l, r, start=True, stop=True):
                return nc.tensor.matmul(o, l, r, start=start, stop=stop)

            def transposes(src, dst):
                for t in range(4):
                    last = nc.tensor.transpose(dst[:, t * P:(t + 1) * P], src[:, t, :], ident[:, :])
                last.then_inc(tr, 1)

            pe.wait_ge(in_w0, 16)
            pe.wait_ge(in_ctxT, 16)
            for b in range(B):
                mm(bank[4 + b], l0w[:, 1, :], ctxT[:, b * S2:(b + 1) * S2]).then_inc(k0_ps, 1)
            for i in range(2):
                for c in range(4):
                    ct = 4 * i + c
                    last = mm(bank[2 + i][:, c * D:(c + 1) * D], ctxT[:, ct * P:(ct + 1) * P], l0w[:, 2, :])
                last.then_inc(v0_ps, 1)
            pe.wait_ge(consts, 1)
            pe.wait_ge(normed, 1)
            transposes(y, bank[7])
            pe.wait_ge(yT_sb, 1)
            mm(bank[6], l0w[:, 0, :], yT[:, :]).then_inc(q0_ps, 1)
            pe.wait_ge(normed, 2)
            transposes(ctx_tok[:, 0:4, :], bank[0])
            transposes(ctx_tok[:, 4:8, :], bank[1])
            pe.wait_ge(in_wv, 16)
            pe.wait_ge(v0_sb, 2)
            for n in range(2 * CT):
                pe.wait_ge(ctxn, 2)
                if n >= 4:
                    pe.wait_ge(v1_sb, n - 3)
                mm(bank[n % 4], ctxT[:, (n // 2) * P:(n // 2 + 1) * P],
                   wv1[:, 512 * (n % 2):512 * (n % 2) + 512]).then_inc(v1_ps, 1)

            mx = 0
            for item in order0:
                if item[0] == "mx":
                    _, b, h, t = item
                    if h == 0 and t == 0:
                        pe.wait_ge(stack[b], 16 * 12)
                        if b == 0:
                            pe.wait_ge(stack_m, 16 * 3)
                    mx += 1
                    if mx > 2:
                        pe.wait_ge(mx_done, mx - 2)
                    q0 = b * S + t * P
                    mm(bank[4 + mx % 2], Qs[:, h, q0:q0 + P], Ks[:, h, b * S2:(b + 1) * S2]).then_inc(mx_ps, 1)
                elif item[0] == "mt":
                    b = item[1]
                    pe.wait_ge(mx_done, (b + 1) * H * QT)
                    if b:
                        pe.wait_ge(mt_parts, b)
                    nc.tensor.transpose(bank[7][0:QT * H, 0:P], nmax[:, b, :, :].rearrange("p t h -> p (t h)"),
                                        ident[:, :]).then_inc(mt_ps, 1)
                elif item[0] == "st":
                    u = item[1]
                    b, h = u // H, u % H
                    if h == 0:
                        pe.wait_ge(max_rows[b], 16 * 6)
                    if u == 0:
                        pe.wait_ge(v1_sb, 2 * CT)
                    if u >= 2:
                        pe.wait_ge(st_exp, u - 1)
                    for k in range(KT):
                        k0 = b * S2 + k * P
                        last = mm(st2[u % 2][:, k * S:(k + 1) * S], Ks[:, h, k0:k0 + P], Qs[:, h, b * S:(b + 1) * S])
                    last.then_inc(st_ps, 1)
                else:
                    g = item[1]
                    b = g // G
                    pe.wait_ge(st_exp, 4 * g + 4)
                    if g == 0:
                        pe.wait_ge(parts, 1)
                    else:
                        pe.wait_ge(o0_sb, g)
                    for k in range(KT):
                        for j in range(4):
                            u = 4 * g + j
                            last = mm(bank[6][32 * j:32 * j + DK0 + 1, 0:S], v0[:, b * KT + k, u % H, :],
                                      prob[:, u % RING, k * S:(k + 1) * S], start=(k == 0), stop=(k == KT - 1))
                    last.then_inc(pv0, 1)

            pe.wait_ge(o0_sb, B * G)
            for t in range(TT):
                b, half = t // QT, t % QT
                for g in range(G):
                    last = nc.tensor.transpose(bank[t][:, g * P:(g + 1) * P], o0[:, b * G + g, half * P:(half + 1) * P],
                                               ident[:, :])
                last.then_inc(t1_ps, 1)
            for t in range(TT):
                pe.wait_ge(on_sb, t + 1)
                last = nc.tensor.transpose(bank[7][:, t * P:(t + 1) * P], on0[:, t, :, :].rearrange("p h d -> p (h d)"),
                                           ident[:, :])
            last.then_inc(t2_ps, 1)
            pe.wait_ge(oT_sb, 1)
            for t in range(TT):
                last = mm(bank[6][:, t * D:(t + 1) * D], oT0[:, t * P:(t + 1) * P], l0w[:, 3, :])
            last.then_inc(wo0_ps, 1)

            pe.wait_ge(normed, 3)
            transposes(y, bank[7])
            pe.wait_ge(in_small, 16 * 8)
            pe.wait_ge(yT_sb, 2)
            for t in range(TT):
                last = mm(bank[6][:, t * E:(t + 1) * E], yT[:, t * P:(t + 1) * P], wr[:, :])
            last.then_inc(rt_ps, 1)
            pe.wait_ge(in_w1, 16)
            pe.wait_ge(in_w2, 16)
            pe.wait_ge(in_wk, 16)

            def hidden(e):
                for f in range(FT):
                    n = e * FT + f
                    if n >= 4:
                        pe.wait_ge(h_sb, n - 3)
                    mm(bank[n % 4], w1[:, e, f * P:(f + 1) * P], yT[:, :]).then_inc(h_ps, 1)

            def rotary(n):
                g, b = n // B, n % B
                if n == 0:
                    pe.wait_ge(rt_wT, 1)
                else:
                    pe.wait_ge(rot_m, n)
                for part in range(2):
                    last = mm(bank[6 + part], wk1[:, 2 * g + part, :], ctxT[:, b * S2:(b + 1) * S2])
                last.then_inc(kp_ps, 1)

            hidden(0)
            pe.wait_ge(rt_w, 1)
            for t in range(TT):
                last = nc.tensor.transpose(bank[7][0:E, t * P:(t + 1) * P], wgt[:, t, :], ident[:, :])
            last.then_inc(rt_wps, 1)
            pe.wait_ge(rt_wT, 1)
            for t in range(TT):
                last = mm(bank[4][:, t * D:(t + 1) * D], wT[:, t * P:(t + 1) * P], b2[:, :])
            last.then_inc(rt_b2, 1)
            for e in range(E):
                rotary(e)
                if e + 1 < E:
                    hidden(e + 1)
                pe.wait_ge(h_sb, FT * (e + 1))
                if e >= 2:
                    pe.wait_ge(y_acc, e - 1)
                elif e == 0:
                    pe.wait_ge(b2_sb, 1)
                for t in range(TT):
                    for f in range(FT):
                        last = mm(bank[4 + e % 2][:, t * D:(t + 1) * D], hT[:, e % 2, f, t * P:(t + 1) * P],
                                  w2[:, e, f, :], start=(f == 0), stop=(f == FT - 1))
                last.then_inc(y_ps, 1)

            pe.wait_ge(normed, 5)
            transposes(y, bank[7])
            pe.wait_ge(yT_sb, 3)
            pe.wait_ge(in_wq, 16)
            for p in range(PAIRS):
                if p >= 2:
                    pe.wait_ge(q1_sb, p - 1)
                mm(bank[4 + p % 2], wq1[:, p * P:(p + 1) * P], yT[:, :]).then_inc(q1_ps, 1)
            for i in range(2):
                pe.wait_ge(rkey_out[i], 16 * 8 * G)
            pe.wait_ge(in_wo, 16)

            def outputs(n):
                b, p = n // PAIRS, n % PAIRS
                pe.wait_ge(clipped, 2 * n + 2)
                if n >= 2:
                    pe.wait_ge(o1_sb, n - 1)
                dst = bank[4 + n % 2]
                for k in range(KT):
                    for e in range(2):
                        h = 2 * p + e
                        mm(dst[64 * e:64 * e + 64, 0:S], v1[:, b * KT + k, h * DK1:(h + 1) * DK1],
                           prob[:, (2 * n + e) % RING, k * S:(k + 1) * S], start=(k == 0), stop=(k == KT - 1))
                for k in range(KT):
                    for e in range(2):
                        last = mm(dst[64 * e:64 * e + 64, S:2 * S], ones[:, 0:64],
                                  prob[:, (2 * n + e) % RING, k * S:(k + 1) * S], start=(k == 0), stop=(k == KT - 1))
                last.then_inc(pv1, 1)

            def project(b):
                pe.wait_ge(o1_sb, PAIRS * (b + 1))
                for t in range(b * QT, (b + 1) * QT):
                    for p in range(PAIRS):
                        last = mm(bank[6][:, t * D:(t + 1) * D], oT1[:, p, t * P:(t + 1) * P], wo1[:, p, :],
                                  start=(p == 0), stop=(p == PAIRS - 1))
                    last.then_inc(wo1_ps, 1)

            for u in range(UNITS):
                b, h = u // H, u % H
                p, e = h // 2, h % 2
                if h % 2 == 0 and b == 0:
                    pe.wait_ge(q1_sb, PAIRS)
                if u >= 2:
                    pe.wait_ge(st_exp, UNITS + u - 1)
                for k in range(KT):
                    k0 = b * S2 + k * P
                    last = mm(st2[u % 2][:, k * S:(k + 1) * S], kT1[64 * e:64 * e + 64, p, k0:k0 + P],
                              qT1[64 * e:64 * e + 64, p, b * S:(b + 1) * S])
                last.then_inc(st_ps, 1)
                if u % 2 == 1 and u >= 3:
                    outputs(u // 2 - 1)
            outputs(UNITS // 2 - 1)
            project(0)
            project(1)

            pe.wait_ge(sc_sb, 1)
            mm(bank[7][:, 0:1], ones[:, :], sc[:, 1:2]).then_inc(sc_ps, 1)
            pe.wait_ge(sc_sb, 2)
            nc.tensor.transpose(bank[7][0:1, 0:P], sc[:, 0:1], ident[:, :]).then_inc(sc_ps, 1)
            pe.wait_ge(sc_sb, 3)
            mm(bank[7][:, 0:1], ones[0:1, :], sc[0:1, 1:2]).then_inc(sc_ps, 1)
            pe.wait_ge(qz_sb, 1)
            for t in range(TT):
                last = nc.tensor.transpose(bank[4].bitcast(bf16)[:, t * P:(t + 1) * P], qzb[:, t, :], identb[:, :])
            last.then_inc(qz_ps, 1)
            pe.wait_ge(qzT_sb, 1)
            for t in range(TT):
                last = mm(bank[6][:, t * D:(t + 1) * D], qzT[:, t * P:(t + 1) * P], qw[:, 0, :])
            last.then_inc(f_ps, 1)


def kernel(**inputs):
    import concourse.bacc as bacc
    from concourse.bass_utils import run_bass_kernel_spmd

    v = {n: np.asarray(a) for n, a in inputs.items()}
    dh = np.arange(D).reshape(H, DK0).T.reshape(-1)
    wkv = v["L1_xattn_Wkv"]
    wk = wkv[:, :H * DK1].reshape(D, G, 4, 2, 32).transpose(0, 1, 3, 2, 4).reshape(D, H * DK1)
    arrays = {
        "x": v["x"].reshape(TT, P, D),
        "ctx": v["ctx_1024"].reshape(CT, P, D),
        "ctxT": v["ctx_1024"].reshape(C, D).T,
        "mask": v["mask_BxS2_bf1"].reshape(1, C).view(np.uint8),
        "l0w": np.stack([v["L0_xattn_Wq"].T[:, dh], v["L0_xattn_Wk"].T[:, dh], v["L0_xattn_Wv"].T, v["L0_xattn_Wo"].T]),
        "bias0": v["L0_xattn_bo"].reshape(1, D),
        "bias1": v["L1_xattn_bo"].reshape(1, D),
        "bias2": v["L1_ffn_bias"].reshape(1, D),
        "brow": v["L0_ffn_b_router"].reshape(1, E),
        "lncol": np.stack([v["L1_xattn_ln_lat_g"], v["L1_xattn_ln_lat_b"], v["L1_xattn_ln_ctx_g"], v["L1_xattn_ln_ctx_b"]], axis=1),
        "wr": v["L0_ffn_W_router"], "w1": v["L0_ffn_W1"], "b1": v["L0_ffn_b1"].reshape(E, FT, P).transpose(2, 0, 1), "w2": v["L0_ffn_W2"], "b2": v["L0_ffn_b2"],
        "cosT": v["L1_xattn_cos"].T, "sinT": v["L1_xattn_sin"].T,
        "wq1": v["L1_xattn_Wq"], "wk1": wk, "wv1": wkv[:, H * DK1:], "wo1": v["L1_xattn_Wo"],
        "wf": v["L1_ffn_weight"].T,
    }
    arrays = {n: np.ascontiguousarray(a) for n, a in arrays.items()}
    nc = bacc.Bacc("TRN2", target_bir_lowering=False, num_devices=1)
    aps = {n: nc.dram_tensor("in_" + n, a.shape, mybir.dt.from_np(a.dtype), kind="ExternalInput").ap()
           for n, a in arrays.items()}
    out = nc.dram_tensor("out_0", (TT, P, D), mybir.dt.float32, kind="ExternalOutput").ap()
    build(nc, aps, out)
    r = run_bass_kernel_spmd(nc, [{"in_" + n: a for n, a in arrays.items()}], core_ids=[0])
    return r.results[0]["out_0"].reshape(B, S, D)
```

```python
import math
from contextlib import ExitStack

import numpy as np

import concourse.bass as bass
from concourse import mybir

P = 128
B, S, S2, D = 2, 256, 512, 128
T, C = B * S, B * S2
TT, CT = T // P, C // P
QT, KT = S // P, S2 // P
H = 16
DK0 = D // H
DK1 = 64
PAIRS = H // 2
G = H // 4
E, FF, FT = 8, 4 * D, 4
NPART = 3
ROWS = NPART * NPART * DK0
MASK_ROW = ROWS
MAX_ROW = 96
NEG = 1.0e10
EPS = 1e-5
CLIP = 11.0
RING = 8
UNITS = B * H
ONE_ONE = float(np.uint32(0x3F803F80).view(np.float32))
MAGIC = 1.5 * 2.0 ** 23


def build(nc, a, out):
    f32, bf16, u8 = mybir.dt.float32, mybir.dt.bfloat16, mybir.dt.uint8
    ALU, ACT, AX = mybir.AluOpType, mybir.ActivationFunctionType, mybir.AxisListType

    ctx = ExitStack()
    with ctx:
        def sb(name, shape, dt=f32):
            return ctx.enter_context(nc.sbuf_tensor(name, shape, dt))

        def sem(name):
            return ctx.enter_context(nc.semaphore(name))

        k_scr = nc.dram_tensor("k_scr", (B, NPART, P, S2), bf16, kind="Internal").ap()
        q_scr = nc.dram_tensor("q_scr", (B, NPART, P, S), bf16, kind="Internal").ap()
        m_scr = nc.dram_tensor("m_scr", (NPART, C), bf16, kind="Internal").ap()

        reg_k = sb("reg_k", [P, 8192])
        Ks = reg_k[:, :].bitcast(bf16).rearrange("p (b h t) -> p b h t", b=B, h=H)
        kT1 = reg_k[:, :].rearrange("p (b a t) -> p b a t", b=B, a=PAIRS)
        reg_q = sb("reg_q", [P, 4096])
        Qs = reg_q[:, :].bitcast(bf16).rearrange("p (b h t) -> p b h t", b=B, h=H)
        qT1 = reg_q[:, :].rearrange("p (b a t) -> p b a t", b=B, a=PAIRS)
        reg_p = sb("reg_p", [P, RING * 1024])
        prob = reg_p[:, :].rearrange("p (r n) -> p r n", r=RING)
        rot = reg_p[:, 0:4096].rearrange("p (r n) -> p r n", r=8)
        rkey = reg_p[:, 4096:6144].rearrange("p (r n) -> p r n", r=4)
        qz = reg_p[:, 0:512].rearrange("p (t d) -> p t d", t=TT)
        qzb = reg_p[:, 512:768].bitcast(bf16).rearrange("p (t d) -> p t d", t=TT)
        qzT = reg_p[:, 768:1024].bitcast(bf16)
        reg_z = sb("reg_z", [P, 4096])
        kf = reg_z[:, 0:1024]
        qf = reg_z[:, 1024:1536]
        res = reg_z[:, 1536:2048]
        res2 = res[:, 0:S]
        kparts = reg_z[:, 2048:2048 + 768].bitcast(bf16).rearrange("p (j t) -> p j t", j=NPART)
        qparts = reg_z[:, 2816:2816 + 384].bitcast(bf16).rearrange("p (j t) -> p j t", j=NPART)
        kparts1 = reg_z[:, 3200:3200 + 768].bitcast(bf16).rearrange("p (j t) -> p j t", j=NPART)
        reg_y = sb("reg_y", [P, 384])
        qparts1 = reg_y[:, :].bitcast(bf16).rearrange("p (j t) -> p j t", j=NPART)
        o0 = reg_z[:, 0:2048].rearrange("p (g q) -> p g q", g=B * G)
        hT = reg_z[:, 2048:4096].rearrange("p (r f t) -> p r f t", r=2, f=FT)
        oT1 = reg_z[:, :].rearrange("p (a t) -> p a t", a=PAIRS)
        w1 = sb("w1", [P, E, FF])
        w2 = sb("w2", [P, E, FT, D])
        wv1 = reg_p[:, 7168:8192]
        wo1 = w1[:, 0:2, :].rearrange("p e (a d) -> p (e a) d", a=PAIRS // 2)
        v1 = sb("v1", [P, CT, H * DK1])
        v0 = sb("v0", [P, CT, H, DK0 + 1])
        ctx_tok = sb("ctx_tok", [P, CT, D])
        wq1 = ctx_tok[:, :, :].rearrange("p c d -> p (c d)")
        ctxT = sb("ctxT", [P, C])
        x = sb("x", [P, TT, D])
        xb = sb("xb", [P, TT, D])
        y = sb("y", [P, TT, D])
        yT = sb("yT", [P, T])
        l0w = sb("l0w", [P, 4, D])
        wk1 = sb("wk1", [P, 2 * G, P])
        sums = ctxT[:, :].rearrange("p (r q) -> p r q", r=4)
        cosT = sb("cosT", [P, S2])
        half_sums = cosT[:, :].rearrange("p (k q) -> p k q", k=2)
        sinT = sb("sinT", [P, S2])
        maskb = sb("maskb", [P, C], u8)
        mask16 = sb("mask16", [16, C // 16], u8)
        mval = sb("mval", [16, 2, C // 16])
        mpart = sb("mpart", [16, NPART, C // 16], bf16)
        bias0, bias1, bias2 = (sb(n, [P, D]) for n in ("bias0", "bias1", "bias2"))
        lncol = sb("lncol", [P, 4])
        wr = sb("wr", [P, E])
        brow = sb("brow", [P, E])
        b1 = sb("b1", [P, E, FT])
        b2 = sb("b2", [E, D])
        wf = sb("wf", [P, D])
        ident = sb("ident", [P, P])
        identb = sb("identb", [P, P], bf16)
        ones = sb("ones", [P, P])
        tri = sb("tri", [P, E, E])
        mhalf = sb("mhalf", [P, 1])
        onesb = sb("onesb", [NPART, P], bf16)
        scr1 = sb("scr1", [P, 1])
        st = sb("st", [P, CT, 6])
        mv = sb("mv", [P, CT, 2])
        ve = sb("ve", [P, CT])
        rstd = sb("rstd", [P, CT])
        nmax = sb("nmax", [P, 2 * B, QT * H // 2])
        maxres = sb("maxres", [H, P])
        maxpart = sb("maxpart", [H, 2 * B, NPART, P], bf16)
        rs0 = sb("rs0", [P, TT, H])
        rs1 = sb("rs1", [P, 2, S])
        on0 = rs1[:, :, :].rearrange("p r (h d) -> p (r h) d", h=2 * H).rearrange("p (t h) d -> p t h d", t=TT)
        wT = rs1[0:E, :, :].rearrange("p r q -> p (r q)")
        oT0 = yT
        gt = sb("gt", [P, QT, E, E])
        eq = sb("eq", [P, QT, E, E])
        lg = sb("lg", [P, TT, E])
        rank = sb("rank", [P, TT, E])
        top = sb("top", [P, TT])
        ex = sb("ex", [P, TT, E])
        wgt = sb("wgt", [P, TT, E])
        qw = sb("qw", [P, 2, D], bf16)
        sc = sb("sc", [P, 8])

        st2 = [ctx.enter_context(nc.psum_tensor(f"st{i}", [P, 1024], f32)) for i in range(2)]
        b4, b5, b6, b7 = (ctx.enter_context(nc.psum_tensor(f"b{i}", [P, 512], f32)) for i in (4, 5, 6, 7))
        bank = [st2[0][:, 0:512], st2[0][:, 512:1024], st2[1][:, 0:512], st2[1][:, 512:1024],
                b4[:, :], b5[:, :], b6[:, :], b7[:, :]]

        in_x, in_w0, in_ctxT, in_mask, in_ctx, in_cols, in_wv, in_rope, in_wk, in_small, in_w1, in_w2, \
            in_wq, in_wo, in_wf = (sem("in_" + n) for n in (
                "x", "w0", "ctxT", "mask", "ctx", "cols", "wv", "rope", "wk", "small", "w1", "w2", "wq", "wo", "wf"))
        consts = sem("consts")
        pool_step = sem("pool_step")
        stats = sem("stats")
        pow_done = sem("pow_done")
        dve_step = sem("dve_step")
        normed = sem("normed")
        tr = sem("tr")
        k0_ps, q0_ps, v0_ps = sem("k0_ps"), sem("q0_ps"), sem("v0_ps")
        q0_f, v0_sb = sem("q0_f"), sem("v0_sb")
        parts = sem("parts")
        mparts = sem("mparts")
        scr_k, scr_q = sem("scr_k"), sem("scr_q")
        scr_m = sem("scr_m")
        stack = [sem(f"stack{b}") for b in range(B)]
        ctxn = sem("ctxn")
        v1_ps, v1_sb = sem("v1_ps"), sem("v1_sb")
        mx_ps, mx_done = sem("mx_ps"), sem("mx_done")
        misc_ps, misc_done = sem("misc_ps"), sem("misc_done")
        mt_parts = sem("mt_parts")
        max_rows = [sem(f"max_rows{q}") for q in range(2 * B)]
        st_ps, st_exp = sem("st_ps"), sem("st_exp")
        clipped, summed = sem("clipped"), sem("summed")
        pv0, o0_sb = sem("pv0"), sem("o0_sb")
        yT_sb = sem("yT_sb")
        rt_lg, rt_ex, rt_w, x_b2 = sem("rt_lg"), sem("rt_ex"), sem("rt_w"), sem("x_b2")
        h_ps, h_sb, y_ps, y_acc = sem("h_ps"), sem("h_sb"), sem("y_ps"), sem("y_acc")
        kp_ps, rot_m, rkey_sb = sem("kp_ps"), sem("rot_m"), sem("rkey_sb")
        rkey_out = [sem(f"rkey_out{i}") for i in range(2)]
        xbias, x_new = sem("xbias"), sem("x_new")
        q1_sb, latT_sb = sem("q1_sb"), sem("latT_sb")
        pv1, o1_sb = sem("pv1"), sem("o1_sb")
        sc_ps, sc_sb = sem("sc_ps"), sem("sc_sb")
        qz_sb, qz_ps, qzT_sb, f_ps, fin = (sem(n) for n in ("qz_sb", "qz_ps", "qzT_sb", "f_ps", "fin"))
        stored = sem("stored")

        block = ctx.enter_context(nc.Block())

        order = []
        maxima = [("mx", q, i) for q in range(2 * B) for i in range(H)]

        def next_maxima(n):
            for _ in range(min(n, len(maxima))):
                order.append(maxima.pop(0))
                if order[-1][2] == 1 and order[-1][1]:
                    order.append(("mt", order[-1][1] - 1))
            if order[-1][0] == "st" and ("mt", 2 * B - 1) not in order:
                order.append(("mt", 2 * B - 1))

        for i in range(CT):
            next_maxima(2)
            order.append(("v1", CT + i))
        next_maxima(8)
        tail = [[("t1", b * QT), ("t1", b * QT + 1), ("t2", b), ("wo", b), ("yt", b), ("rt", b), ("wt", b), ("b2", b)]
                for b in range(B)]
        left = list(tail[0])
        for u in range(UNITS):
            order.append(("st", u))
            next_maxima(1)
            if u > 4 and u % 4:
                order.append(("pv", u // 4 - 1, u % 4 - 1))
            next_maxima(1)
            if u > 4 and u % 4 == 3:
                order.append(("pv", u // 4 - 1, 3))
            if u >= H + 3 and left:
                order.append(left.pop(0))
        order += [("pv", 2 * G - 1, k) for k in range(KT)]
        order += left
        order.append(("hid", 0))
        left = list(tail[1])
        for n in range(B * E):
            if n + 1 < B * E:
                order.append(("hid", n + 1))
            if n % 2 == 1:
                order.append(("kp", n // 2))
            order.append(("yy", n))
            if n == E - 1:
                order.append(("ln1", 0))
            if n < E:
                order.append(left.pop(0))
            if n == E + 1:
                order.append(("l1t", 0))
            if E + 2 <= n < E + 6:
                order.append(("q1", 0, n - E - 2))
        for u in range(UNITS):
            order.append(("s1", u))
            if u % 2 == 1 and u >= 3:
                order.append(("o1", u // 2 - 1))
            if u == 0:
                order.append(("ln1", 1))
            if u == 4:
                order.append(("l1t", 1))
            if 6 <= u < 10:
                order.append(("q1", 1, u - 6))
            if u == H + 4:
                order.append(("w1o", 0))
        order += [("o1", UNITS // 2 - 1), ("w1o", 1)]
        misc = {}
        norm = {}
        for item in order:
            if item[0] in ("mt", "t1", "t2", "wo", "yt", "rt", "wt", "b2", "kp", "l1t", "q1", "w1o"):
                misc[item] = len(misc) + 1
            if item[0] in ("wo", "ln1", "w1o"):
                norm[item] = 3 + sum(2 if k[0] == "ln1" else 1 for k in norm)

        @block.sync
        def _(sp):
            def load(dst, src, s):
                sp.dma_start(dst, src).then_inc(s, 16)

            load(x[:, :, :], a["x"].rearrange("t p d -> p t d"), in_x)
            load(ctxT[:, :], a["ctxT"], in_ctxT)
            load(l0w[:, :, :], a["l0w"].rearrange("n p d -> p n d"), in_w0)
            load(ctx_tok[:, :, :], a["ctx"].rearrange("t p d -> p t d"), in_ctx)
            load(mask16[:, :], a["mask"].rearrange("a (p n) -> (a p) n", p=16), in_mask)
            load(maskb[:, :], a["mask"].broadcast_to([P, C]), in_mask)
            sp.wait_ge(mparts, 1)
            sp.dma_start(m_scr.rearrange("j (p n) -> p j n", p=16), mpart[:, :, :]).then_inc(scr_m, 16)
            for b in range(B):
                kp = kparts if b == 0 else kparts1
                qp = qparts if b == 0 else qparts1
                sp.wait_ge(consts, b + 2)
                sp.dma_start(Ks[MAX_ROW:MAX_ROW + NPART, b, :, :].rearrange("j h (k n) -> j (h k) n", n=P),
                             onesb[:, None, :].broadcast_to([NPART, H * KT, P])).then_inc(stack[b], 16)
                if b == 0:
                    sp.wait_ge(scr_m, 16)
                sp.dma_start(Ks[MASK_ROW:MASK_ROW + NPART, b, :, :],
                             m_scr[:, None, b * S2:(b + 1) * S2].broadcast_to([NPART, H, S2])).then_inc(stack[b], 16)
                sp.wait_ge(parts, 2 * b + 1)
                sp.dma_start(k_scr[b].rearrange("j p t -> p j t"), kp).then_inc(scr_k, 16)
                sp.wait_ge(parts, 2 * b + 2)
                sp.dma_start(q_scr[b].rearrange("j p t -> p j t"), qp).then_inc(scr_q, 16)
                sp.wait_ge(scr_k, 16 * (b + 1))
                for i in range(NPART):
                    r = i * NPART * DK0
                    sp.dma_start(Ks[r:r + NPART * DK0, b, :, :],
                                 k_scr[b].rearrange("j (d h) t -> (j d) h t", h=H)).then_inc(stack[b], 16)
                sp.wait_ge(scr_q, 16 * (b + 1))
                for i in range(NPART):
                    r = i * NPART * DK0
                    for j in range(NPART):
                        sp.dma_start(Qs[r + j * DK0:r + (j + 1) * DK0, b, :, :],
                                     q_scr[b, i].rearrange("(d h) t -> d h t", h=H)).then_inc(stack[b], 16)
            for q in range(4):
                load(cosT[32 * q:32 * q + 32, :], a["cosT"], in_rope)
                load(sinT[32 * q:32 * q + 32, :], a["sinT"], in_rope)
            load(wk1[:, :, :], a["wk1"].rearrange("p (n c) -> p n c", n=2 * G), in_wk)
            for q in range(2 * B):
                b, h0 = q // 2, 8 * (q % 2)
                sp.wait_ge(mt_parts, q + 1)
                for j in range(NPART):
                    sp.dma_start(Qs[MAX_ROW + j:MAX_ROW + j + 1, b, h0:h0 + 8, :].rearrange("j h (t n) -> j (h t) n", t=QT),
                                 maxpart[:, q, j, :]).then_inc(max_rows[q], 16)
                if q == 0:
                    load(w1[:, :, :], a["w1"].rearrange("e p f -> p e f"), in_w1)
                elif q == 1:
                    load(w2[:, :, :, :], a["w2"].rearrange("e (f p) d -> p e f d", p=P), in_w2)
            sp.wait_ge(tr, 3)
            sp.dma_start(wq1, a["wq1"]).then_inc(in_wq, 16)
            sp.wait_ge(st_ps, UNITS)
            for n in range(B * G):
                b, g = n // G, n % G
                sp.wait_ge(rkey_sb, 2 * (n + 1))
                for part in range(2):
                    for j in range(4):
                        head = 4 * g + j
                        r = 64 * (head % 2) + 32 * part
                        sp.dma_start(kT1[r:r + 32, b, head // 2, :],
                                     rkey[32 * j:32 * j + 32, 2 * (n % 2) + part, :]).then_inc(rkey_out[n % 2], 16)
            sp.wait_ge(h_ps, B * E * FT)
            sp.dma_start(wo1, a["wo1"].rearrange("(a p) d -> p a d", p=P)).then_inc(in_wo, 16)
            sp.wait_ge(fin, 1)
            sp.dma_start(out.rearrange("t p d -> p t d"), qz[:, :, :]).then_inc(stored, 16)
            sp.wait_ge(stored, 16)

        @block.gpsimd
        def _(pool):
            steps = [0]

            def link(ins):
                steps[0] += 1
                ins.then_inc(pool_step, 1)
                pool.wait_ge(pool_step, steps[0])

            nc.gpsimd.memset(mhalf[:, :], -0.5)
            nc.gpsimd.memset(ones[:, :], 1.0)
            nc.gpsimd.memset(onesb[:, :], 1.0)
            nc.gpsimd.memset(tri[:, :, :], 1.0)
            link(nc.gpsimd.memset(ident[:, :], 0.0))
            link(nc.gpsimd.affine_select(out=ident[:, :], in_=ident[:, :], compare_op=ALU.not_equal, fill=1.0,
                                         base=0, pattern=[[-1, P]], channel_multiplier=1))
            link(nc.gpsimd.tensor_copy(identb[:, :], ident[:, :]))
            nc.gpsimd.affine_select(out=tri[:, :, :], in_=tri[:, :, :], compare_op=ALU.is_ge, fill=0.0,
                                    base=-1, pattern=[[1, E], [-1, E]], channel_multiplier=0).then_inc(consts, 1)
            pool.wait_ge(consts, 1)
            link(nc.gpsimd.memset(reg_k[64:128, 0:4096], 0.0))
            powers = [0]

            def power(tiles):
                powers[0] += 1
                pool.wait_ge(stats, powers[0])
                nc.gpsimd.tensor_tensor(rstd[:, 0:tiles], ve[:, 0:tiles], mhalf[:, :].broadcast_to([P, tiles]),
                                        ALU.pow).then_inc(pow_done, 1)

            power(TT)
            pool.wait_ge(in_mask, 32)
            link(nc.gpsimd.tensor_scalar(mval[:, 0, :], mask16[:, :], NEG, NEG, ALU.mult, ALU.subtract))
            link(nc.gpsimd.tensor_copy(mpart[:, 0, :], mval[:, 0, :]))
            link(nc.gpsimd.tensor_tensor(mval[:, 1, :], mval[:, 0, :], mpart[:, 0, :], ALU.subtract))
            link(nc.gpsimd.tensor_copy(mpart[:, 1, :], mval[:, 1, :]))
            nc.gpsimd.tensor_tensor(mpart[:, 2, :], mval[:, 1, :], mpart[:, 1, :], ALU.subtract).then_inc(mparts, 1)
            pool.wait_ge(mparts, 1)
            nc.gpsimd.memset(reg_q[64:128, 0:2048], ONE_ONE).then_inc(consts, 1)
            pool.wait_ge(consts, 2)
            power(CT)
            pool.wait_ge(pow_done, 2)
            link(nc.gpsimd.memset(v0[:, :, :, DK0:DK0 + 1], 1.0))
            link(nc.gpsimd.memset(reg_q[64:128, 2048:4096], ONE_ONE))
            nc.gpsimd.memset(reg_k[64:128, 4096:8192], 0.0).then_inc(consts, 1)
            pool.wait_ge(consts, 3)
            pool.wait_ge(in_small, 16 * 8)
            nc.gpsimd.tensor_tensor(xb[:, :, :], x[:, :, :], bias0[:, None, :].broadcast_to([P, TT, D]),
                                    ALU.add).then_inc(xbias, 1)
            for item in order:
                kind = item[0]
                if kind == "wo":
                    power(QT)
                elif kind == "ln1":
                    b = item[1]
                    power(QT)
                    power(QT)
                    pool.wait_ge(x_new, B + b + 1)
                    nc.gpsimd.tensor_tensor(xb[:, b * QT:(b + 1) * QT, :], x[:, b * QT:(b + 1) * QT, :],
                                            bias1[:, None, :].broadcast_to([P, QT, D]), ALU.add).then_inc(xbias, 1)
                elif kind == "kp":
                    n = item[1]
                    pool.wait_ge(rot_m, n + 1)
                    if n >= 2:
                        pool.wait_ge(rkey_out[n % 2], 16 * 8 * (n // 2))
                    q4 = 4 * (n % 2)
                    nc.gpsimd.tensor_tensor(rkey[:, 2 * (n % 2), :], rot[:, q4, :], rot[:, q4 + 1, :],
                                            ALU.subtract).then_inc(rkey_sb, 1)
                    nc.gpsimd.tensor_tensor(rkey[:, 2 * (n % 2) + 1, :], rot[:, q4 + 2, :], rot[:, q4 + 3, :],
                                            ALU.add).then_inc(rkey_sb, 1)
                elif kind == "s1":
                    u = item[1]
                    pool.wait_ge(clipped, u + 1)
                    if u:
                        pool.wait_ge(summed, u)
                    p4 = prob[:, u % RING, :].rearrange("p (k q) -> p k q", k=KT)
                    link(nc.gpsimd.tensor_tensor(half_sums, p4[:, 0:2, :], p4[:, 2:4, :], ALU.add))
                    if u >= 4:
                        pool.wait_ge(pv1, (u - 4) // 2 + 1)
                    nc.gpsimd.tensor_tensor(sums[:, u % 4, :], half_sums[:, 0, :], half_sums[:, 1, :],
                                            ALU.add).then_inc(summed, 1)
                elif kind == "w1o":
                    b = item[1]
                    power(QT)
                    pool.wait_ge(x_new, 2 * B + b + 1)
                    nc.gpsimd.tensor_tensor(xb[:, b * QT:(b + 1) * QT, :], x[:, b * QT:(b + 1) * QT, :],
                                            bias2[:, None, :].broadcast_to([P, QT, D]), ALU.add).then_inc(xbias, 1)

        @block.scalar
        def _(act):
            def load(dst, src, s):
                act.dma_start(dst, src).then_inc(s, 16)

            load(wv1, a["wv1"], in_wv)
            load(lncol[:, :], a["lncol"], in_cols)
            for dst, name in ((bias0, "bias0"), (bias1, "bias1"), (bias2, "bias2"), (brow, "brow")):
                load(dst[:, :], a[name].broadcast_to([P, dst.shape[1]]), in_small)
            load(wr[:, :], a["wr"], in_small)
            load(b1[:, :, :], a["b1"], in_small)
            load(b2[:, :], a["b2"], in_small)
            load(wf[:, :], a["wf"], in_small)

            def values(n):
                act.wait_ge(v1_ps, n + 1)
                nc.scalar.activation(v1[:, n // 2, 512 * (n % 2):512 * (n % 2) + 512], bank[n % 4],
                                     ACT.Copy).then_inc(v1_sb, 1)

            act.wait_ge(q0_ps, 1)
            nc.scalar.activation(qf, bank[6], ACT.Copy, scale=1.0 / math.sqrt(DK0)).then_inc(q0_f, 1)
            for i in range(2):
                act.wait_ge(v0_ps, i + 1)
                nc.scalar.activation(v0[:, 4 * i:4 * i + 4, :, 0:DK0],
                                     bank[2 + i].rearrange("p (c h d) -> p c h d", c=4, h=H),
                                     ACT.Copy).then_inc(v0_sb, 1)
            act.wait_ge(in_cols, 16)
            for i in range(2):
                act.wait_ge(tr, 2 + i)
                nc.scalar.activation(ctxT[:, 512 * i:512 * i + 512], bank[i], ACT.Identity,
                                     scale=lncol[:, 2:3], bias=lncol[:, 3:4]).then_inc(ctxn, 1)
            for n in range(CT):
                values(n)
            for item in order:
                kind = item[0]
                if kind == "v1":
                    values(item[1])
                elif kind == "st":
                    u = item[1]
                    act.wait_ge(st_ps, u + 1)
                    if u >= RING:
                        act.wait_ge(pv0, u // 4 - 1)
                    nc.scalar.activation(prob[:, u % RING, :], st2[u % 2][:, :], ACT.Exp).then_inc(st_exp, 1)
                elif kind == "rt":
                    b = item[1]
                    act.wait_ge(rt_lg, b + 1)
                    nc.scalar.activation(ex[:, b * QT:(b + 1) * QT, :], lg[:, b * QT:(b + 1) * QT, :],
                                         ACT.Exp).then_inc(rt_ex, 1)
                elif kind == "hid":
                    n = item[1]
                    for f in range(FT):
                        act.wait_ge(h_ps, n * FT + f + 1)
                        if n >= 2:
                            act.wait_ge(y_ps, n - 1)
                        nc.scalar.activation(hT[:, n % 2, f, :], bank[f][:, 0:S], ACT.Relu,
                                             bias=b1[:, n % E, f:f + 1]).then_inc(h_sb, 1)
                elif kind == "l1t":
                    b = item[1]
                    act.wait_ge(misc_ps, misc[item])
                    if b == 1:
                        act.wait_ge(misc_ps, misc[("q1", 0, 3)])
                    nc.scalar.activation(yT[:, b * S:(b + 1) * S], bank[7][:, 0:S], ACT.Identity,
                                         scale=lncol[:, 0:1], bias=lncol[:, 1:2]).then_inc(misc_done, 1)
                elif kind == "q1":
                    _, b, i = item
                    act.wait_ge(misc_ps, misc[item])
                    nc.scalar.activation(qT1[:, b, 2 * i:2 * i + 2, :],
                                         bank[7].rearrange("p (a q) -> p a q", a=2), ACT.Copy).then_inc(misc_done, 1)
                elif kind == "s1":
                    u = item[1]
                    act.wait_ge(st_ps, UNITS + u + 1)
                    if u >= RING:
                        act.wait_ge(pv1, u // 2 - 3)
                        act.wait_ge(summed, u - RING + 1)
                    elif u == 0:
                        act.wait_ge(rkey_sb, 2 * B * G)
                    elif u == 4:
                        for i in range(2):
                            act.wait_ge(rkey_out[i], 16 * 8 * G)
                    nc.scalar.activation(prob[:, u % RING, :], st2[u % 2][:, :], ACT.Exp,
                                         scale=DK1 ** -0.5).then_inc(st_exp, 1)

        @block.vector
        def _(dve):
            steps = [0]

            def link(ins):
                steps[0] += 1
                ins.then_inc(dve_step, 1)
                dve.wait_ge(dve_step, steps[0])

            norms = [0]

            def layer_norm(dst, src, first, tiles):
                norms[0] += 1
                for t in range(tiles):
                    last = nc.vector.bn_stats(st[:, t, :], src[:, first + t, :])
                link(last)
                for t in range(tiles):
                    last = nc.vector.bn_aggr(mv[:, t, :], st[:, t, :])
                link(last)
                nc.vector.tensor_scalar_add(ve[:, 0:tiles], mv[:, 0:tiles, 1], EPS).then_inc(stats, 1)
                dve.wait_ge(pow_done, norms[0])
                for t in range(tiles):
                    last = nc.vector.tensor_scalar(dst[:, first + t, :], src[:, first + t, :], mv[:, t, 0:1],
                                                   rstd[:, t:t + 1], ALU.subtract, ALU.mult)
                last.then_inc(normed, 1)

            def split(dst, src, tmp):
                link(nc.vector.tensor_copy(dst[0], src))
                link(nc.vector.tensor_tensor(tmp, src, dst[0], ALU.subtract))
                link(nc.vector.tensor_copy(dst[1], tmp))
                return nc.vector.tensor_tensor(dst[2], tmp, dst[1], ALU.subtract)

            def take(item):
                dve.wait_ge(misc_ps, misc[item])

            dve.wait_ge(in_x, 16)
            layer_norm(y, x, 0, TT)
            dve.wait_ge(in_ctx, 16)
            layer_norm(ctx_tok, ctx_tok, 0, CT)
            dve.wait_ge(tr, 1)
            nc.vector.tensor_copy(yT[:, :], bank[7]).then_inc(yT_sb, 1)
            dve.wait_ge(in_mask, 32)
            for b in range(B):
                dve.wait_ge(k0_ps, b + 1)
                last = nc.vector.tensor_tensor(kf[:, b * S2:(b + 1) * S2], bank[4 + b],
                                               maskb[:, b * S2:(b + 1) * S2], ALU.mult)
            link(last)
            for b in range(B):
                kp = kparts if b == 0 else kparts1
                qp = qparts if b == 0 else qparts1
                split([kp[:, j, :] for j in range(NPART)], kf[:, b * S2:(b + 1) * S2], res).then_inc(parts, 1)
                if b == 0:
                    dve.wait_ge(q0_f, 1)
                dve.wait_ge(parts, 2 * b + 1)
                split([qp[:, j, :] for j in range(NPART)], qf[:, b * S:(b + 1) * S], res2).then_inc(parts, 1)
                dve.wait_ge(parts, 2 * b + 2)
            nc.vector.memset(bank[6], 0.0).then_inc(o0_sb, 1)

            mx = 0
            for item in order:
                kind = item[0]
                if kind == "mx":
                    _, q, i = item
                    mx += 1
                    dve.wait_ge(mx_ps, mx)
                    nc.vector.tensor_reduce(nmax[:, q, i:i + 1], bank[4 + mx % 2], AX.X, ALU.max,
                                            negate=True).then_inc(mx_done, 1)
                elif kind == "mt":
                    q = item[1]
                    take(item)
                    src = bank[7][0:H, 0:P]
                    dst = maxpart[:, q, :, :]
                    link(nc.vector.tensor_copy(dst[:, 0, :], src))
                    nc.vector.tensor_tensor(maxres[:, :], src, dst[:, 0, :], ALU.subtract).then_inc(misc_done, 1)
                    dve.wait_ge(misc_done, misc[item])
                    link(nc.vector.tensor_copy(dst[:, 1, :], maxres[:, :]))
                    nc.vector.tensor_tensor(dst[:, 2, :], maxres[:, :], dst[:, 1, :], ALU.subtract).then_inc(mt_parts, 1)
                elif kind == "pv" and item[2] == KT - 1:
                    g = item[1]
                    dve.wait_ge(pv0, g + 1)
                    if g == 0:
                        dve.wait_ge(stack[1], 16 * 14)
                    nc.vector.tensor_copy(o0[:, g, :], bank[6][:, 0:S]).then_inc(o0_sb, 1)
                elif kind == "t1":
                    t = item[1]
                    take(item)
                    o = bank[7].rearrange("p (h c) -> p h c", h=H)
                    link(nc.vector.reciprocal(rs0[:, t, :], o[:, :, DK0]))
                    nc.vector.tensor_tensor(on0[:, t, :, :], o[:, :, 0:DK0],
                                            rs0[:, t, :, None].broadcast_to([P, H, DK0]), ALU.mult).then_inc(misc_done, 1)
                elif kind == "t2":
                    b = item[1]
                    take(item)
                    nc.vector.tensor_copy(oT0[:, b * S:(b + 1) * S], bank[7][:, 0:S]).then_inc(misc_done, 1)
                elif kind in ("wo", "w1o"):
                    b = item[1]
                    dve.wait_ge(xbias, 1 if kind == "wo" else 1 + B)
                    take(item)
                    nc.vector.tensor_tensor(x[:, b * QT:(b + 1) * QT, :], bank[7][:, 0:S].rearrange("p (t d) -> p t d", t=QT),
                                            xb[:, b * QT:(b + 1) * QT, :], ALU.add).then_inc(misc_done, 1)
                    dve.wait_ge(misc_done, misc[item])
                    nc.vector.tensor_copy(scr1[:, 0:1], x[:, b * QT, 0:1]).then_inc(x_new, 1)
                    layer_norm(y, x, b * QT, QT)
                elif kind == "yt":
                    b = item[1]
                    take(item)
                    nc.vector.tensor_copy(yT[:, b * S:(b + 1) * S], bank[7][:, 0:S]).then_inc(misc_done, 1)
                elif kind == "rt":
                    b = item[1]
                    r = slice(b * QT, (b + 1) * QT)
                    take(item)
                    nc.vector.tensor_tensor(lg[:, r, :], bank[7][:, 0:QT * E].rearrange("p (t e) -> p t e", t=QT),
                                            brow[:, None, :].broadcast_to([P, QT, E]), ALU.add).then_inc(misc_done, 1)
                    dve.wait_ge(misc_done, misc[item])
                    nc.vector.tensor_reduce(top[:, r], lg[:, r, :], AX.X, ALU.max)
                    for t in range(QT):
                        lj = lg[:, b * QT + t, None, :].broadcast_to([P, E, E])
                        le = lg[:, b * QT + t, :, None].broadcast_to([P, E, E])
                        nc.vector.tensor_tensor(gt[:, t, :, :], lj, le, ALU.is_gt)
                        last = nc.vector.tensor_tensor(eq[:, t, :, :], lj, le, ALU.is_equal)
                    link(last)
                    nc.vector.tensor_tensor(lg[:, r, :], lg[:, r, :], top[:, r, None].broadcast_to([P, QT, E]),
                                            ALU.subtract).then_inc(rt_lg, 1)
                    link(nc.vector.tensor_tensor(eq[:, :, :, :], eq[:, :, :, :],
                                                 tri[:, None, :, :].broadcast_to([P, QT, E, E]), ALU.mult))
                    link(nc.vector.tensor_tensor(gt[:, :, :, :], gt[:, :, :, :], eq[:, :, :, :], ALU.add))
                    link(nc.vector.tensor_reduce(rank[:, r, :], gt[:, :, :, :], AX.X, ALU.add))
                    dve.wait_ge(rt_ex, b + 1)
                    link(nc.vector.scalar_tensor_tensor(out=wgt[:, r, :], in0=rank[:, r, :], scalar=2.0, in1=ex[:, r, :],
                                                        op0=ALU.is_lt, op1=ALU.mult))
                    link(nc.vector.tensor_reduce(top[:, r], wgt[:, r, :], AX.X, ALU.add))
                    link(nc.vector.reciprocal(top[:, r], top[:, r]))
                    nc.vector.tensor_tensor(wgt[:, r, :], wgt[:, r, :], top[:, r, None].broadcast_to([P, QT, E]),
                                            ALU.mult).then_inc(rt_w, 1)
                elif kind == "wt":
                    b = item[1]
                    take(item)
                    nc.vector.tensor_copy(wT[:, b * S:(b + 1) * S], bank[7][0:E, 0:S]).then_inc(misc_done, 1)
                elif kind == "b2":
                    b = item[1]
                    take(item)
                    nc.vector.tensor_tensor(x[:, b * QT:(b + 1) * QT, :], bank[7][:, 0:S].rearrange("p (t d) -> p t d", t=QT),
                                            x[:, b * QT:(b + 1) * QT, :], ALU.add).then_inc(misc_done, 1)
                    dve.wait_ge(misc_done, misc[item])
                elif kind == "yy":
                    n = item[1]
                    b, e = n // E, n % E
                    dve.wait_ge(y_ps, n + 1)
                    if n:
                        dve.wait_ge(y_acc, n)
                    for t in range(QT):
                        last = nc.vector.scalar_tensor_tensor(
                            out=x[:, b * QT + t, :], in0=bank[4 + n % 2][:, t * D:(t + 1) * D],
                            scalar=wgt[:, b * QT + t, e:e + 1], in1=x[:, b * QT + t, :], op0=ALU.mult, op1=ALU.add)
                    last.then_inc(y_acc, 1)
                    if e == E - 1:
                        dve.wait_ge(y_acc, n + 1)
                        nc.vector.tensor_copy(scr1[:, 0:1], x[:, b * QT, 0:1]).then_inc(x_new, 1)
                elif kind == "kp":
                    n = item[1]
                    if n == 0:
                        dve.wait_ge(in_rope, 16 * 8)
                    if n >= 2:
                        dve.wait_ge(rkey_sb, 2 * (n - 1))
                    q4 = 4 * (n % 2)
                    take(item)
                    nc.vector.tensor_tensor(rot[:, q4 + 1, :], bank[7], sinT[:, :], ALU.mult)
                    nc.vector.tensor_tensor(rot[:, q4 + 2, :], bank[7], cosT[:, :], ALU.mult).then_inc(misc_done, 1)
                    nc.vector.tensor_tensor(rot[:, q4, :], bank[6], cosT[:, :], ALU.mult)
                    nc.vector.tensor_tensor(rot[:, q4 + 3, :], bank[6], sinT[:, :], ALU.mult).then_inc(rot_m, 1)
                elif kind == "ln1":
                    b = item[1]
                    layer_norm(y, x, b * QT, QT)
                    dve.wait_ge(normed, norm[item])
                    layer_norm(y, y, b * QT, QT)
                elif kind == "s1":
                    u = item[1]
                    dve.wait_ge(st_exp, UNITS + u + 1)
                    nc.vector.tensor_scalar(prob[:, u % RING, :], prob[:, u % RING, :], math.exp(-CLIP),
                                            math.exp(CLIP), ALU.max, ALU.min).then_inc(clipped, 1)
                elif kind == "o1":
                    n = item[1]
                    dve.wait_ge(pv1, n + 1)
                    link(nc.vector.reciprocal(rs1[:, n % 2, :], bank[4 + n % 2][:, S:2 * S]))
                    nc.vector.tensor_tensor(oT1[:, n % PAIRS, (n // PAIRS) * S:(n // PAIRS + 1) * S],
                                            bank[4 + n % 2][:, 0:S], rs1[:, n % 2, :], ALU.mult).then_inc(o1_sb, 1)
                    if n == 3:
                        nc.vector.tensor_reduce(sc[:, 1:2], wf[:, :], AX.X, ALU.add,
                                                apply_absolute_value=True).then_inc(sc_sb, 1)

            dve.wait_ge(sc_ps, 1)
            link(nc.vector.tensor_scalar_mul(sc[:, 2:3], bank[6][:, 0:1], 1.0 / (D * D)))
            dve.wait_ge(normed, norm[("w1o", 1)])
            nc.vector.tensor_reduce(sc[:, 0:1], y[:, :, :], AX.XY, ALU.max, apply_absolute_value=True).then_inc(sc_sb, 1)
            nc.vector.tensor_scalar_mul(sc[:, 4:5], sc[:, 2:3], 0.5)
            link(nc.vector.tensor_scalar_mul(sc[:, 3:4], sc[:, 2:3], -0.5))
            link(nc.vector.tensor_scalar(qw[:, 1, :], wf[:, :], sc[:, 3:4], None, ALU.is_lt))
            link(nc.vector.scalar_tensor_tensor(out=qw[:, 0, :], in0=wf[:, :], scalar=sc[:, 4:5], in1=qw[:, 1, :],
                                                op0=ALU.is_gt, op1=ALU.subtract))
            dve.wait_ge(sc_ps, 2)
            nc.vector.tensor_reduce(sc[0:1, 1:2], bank[7][0:1, 0:P], AX.X, ALU.max).then_inc(sc_sb, 1)
            dve.wait_ge(sc_ps, 3)
            link(nc.vector.tensor_scalar_mul(sc[:, 5:6], bank[7][:, 0:1], 1.0 / 127.0))
            link(nc.vector.reciprocal(sc[:, 6:7], sc[:, 5:6]))
            link(nc.vector.tensor_tensor(sc[:, 7:8], sc[:, 5:6], sc[:, 2:3], ALU.mult))
            link(nc.vector.tensor_scalar_mul(qz[:, :, :], y[:, :, :], sc[:, 6:7]))
            link(nc.vector.tensor_scalar(qz[:, :, :], qz[:, :, :], MAGIC, MAGIC, ALU.add, ALU.subtract))
            nc.vector.tensor_scalar(qzb[:, :, :], qz[:, :, :], -128.0, 127.0, ALU.max, ALU.min).then_inc(qz_sb, 1)
            dve.wait_ge(qz_ps, 1)
            nc.vector.tensor_copy(qzT[:, :], bank[4].bitcast(bf16)[:, 0:T]).then_inc(qzT_sb, 1)
            dve.wait_ge(xbias, 1 + 2 * B)
            dve.wait_ge(f_ps, 1)
            nc.vector.scalar_tensor_tensor(out=qz[:, :, :], in0=bank[6].rearrange("p (t d) -> p t d", t=TT),
                                           scalar=sc[:, 7:8], in1=xb[:, :, :], op0=ALU.mult, op1=ALU.add).then_inc(fin, 1)

        @block.tensor
        def _(pe):
            def mm(o, l, r, start=True, stop=True):
                return nc.tensor.matmul(o, l, r, start=start, stop=stop)

            def transposes(src, first, tiles, dst):
                for t in range(tiles):
                    last = nc.tensor.transpose(dst[:, t * P:(t + 1) * P], src[:, first + t, :], ident[:, :])
                return last

            def values(n):
                if n >= 4:
                    pe.wait_ge(v1_sb, n - 3)
                mm(bank[n % 4], ctxT[:, (n // 2) * P:(n // 2 + 1) * P],
                   wv1[:, 512 * (n % 2):512 * (n % 2) + 512]).then_inc(v1_ps, 1)

            def free(item):
                if misc[item] > 1:
                    pe.wait_ge(misc_done, misc[item] - 1)

            pe.wait_ge(in_w0, 16)
            pe.wait_ge(in_ctxT, 16)
            for b in range(B):
                mm(bank[4 + b], l0w[:, 1, :], ctxT[:, b * S2:(b + 1) * S2]).then_inc(k0_ps, 1)
            pe.wait_ge(consts, 1)
            pe.wait_ge(normed, 1)
            transposes(y, 0, TT, bank[7]).then_inc(tr, 1)
            for i in range(2):
                for c in range(4):
                    ct = 4 * i + c
                    last = mm(bank[2 + i][:, c * D:(c + 1) * D], ctxT[:, ct * P:(ct + 1) * P], l0w[:, 2, :])
                last.then_inc(v0_ps, 1)
            pe.wait_ge(yT_sb, 1)
            mm(bank[6], l0w[:, 0, :], yT[:, :]).then_inc(q0_ps, 1)
            pe.wait_ge(normed, 2)
            for i in range(2):
                transposes(ctx_tok, 4 * i, 4, bank[i]).then_inc(tr, 1)
            pe.wait_ge(in_wv, 16)
            pe.wait_ge(v0_sb, 2)
            pe.wait_ge(ctxn, 2)
            for n in range(CT):
                values(n)

            mx = 0
            for item in order:
                kind = item[0]
                if item in misc:
                    free(item)
                if kind == "v1":
                    values(item[1])
                elif kind == "mx":
                    _, q, i = item
                    b, h, t = q // 2, 8 * (q % 2) + i // 2, i % 2
                    if q % 2 == 0 and i == 0:
                        pe.wait_ge(stack[b], 16 * 14)
                    mx += 1
                    if mx > 2:
                        pe.wait_ge(mx_done, mx - 2)
                    mm(bank[4 + mx % 2], Qs[0:MAX_ROW, b, h, t * P:(t + 1) * P], Ks[0:MAX_ROW, b, h, :]).then_inc(mx_ps, 1)
                elif kind == "mt":
                    q = item[1]
                    pe.wait_ge(mx_done, (q + 1) * H)
                    nc.tensor.transpose(bank[7][0:H, 0:P], nmax[:, q, :],
                                        ident[:, :]).then_inc(misc_ps, 1)
                elif kind == "st":
                    u = item[1]
                    b, h = u // H, u % H
                    if u % 8 == 0:
                        pe.wait_ge(max_rows[u // 8], 16 * NPART)
                    if u == 0:
                        pe.wait_ge(v1_sb, 2 * CT)
                    if u >= 2:
                        pe.wait_ge(st_exp, u - 1)
                    for k in range(KT):
                        last = mm(st2[u % 2][:, k * S:(k + 1) * S], Ks[:, b, h, k * P:(k + 1) * P], Qs[:, b, h, :])
                    last.then_inc(st_ps, 1)
                elif kind == "pv":
                    _, g, k = item
                    b = g // G
                    if k == 0:
                        pe.wait_ge(st_exp, 4 * g + 4)
                        pe.wait_ge(o0_sb, g + 1)
                    for j in range(4):
                        u = 4 * g + j
                        last = mm(bank[6][32 * j:32 * j + DK0 + 1, 0:S], v0[:, b * KT + k, u % H, :],
                                  prob[:, u % RING, k * S:(k + 1) * S], start=(k == 0), stop=(k == KT - 1))
                    if k == KT - 1:
                        last.then_inc(pv0, 1)
                elif kind == "t1":
                    t = item[1]
                    b, half = t // QT, t % QT
                    pe.wait_ge(o0_sb, G * (b + 1) + 1)
                    for g in range(G):
                        last = nc.tensor.transpose(bank[7][:, g * P:(g + 1) * P],
                                                   o0[:, b * G + g, half * P:(half + 1) * P], ident[:, :])
                    last.then_inc(misc_ps, 1)
                elif kind == "t2":
                    b = item[1]
                    for t in range(QT):
                        last = nc.tensor.transpose(bank[7][:, t * P:(t + 1) * P],
                                                   on0[:, b * QT + t, :, :].rearrange("p h d -> p (h d)"), ident[:, :])
                    last.then_inc(misc_ps, 1)
                elif kind == "wo":
                    b = item[1]
                    for t in range(QT):
                        last = mm(bank[7][:, t * D:(t + 1) * D], oT0[:, (b * QT + t) * P:(b * QT + t + 1) * P], l0w[:, 3, :])
                    last.then_inc(misc_ps, 1)
                elif kind in ("yt", "l1t"):
                    b = item[1]
                    pe.wait_ge(normed, norm[("wo", b)] if kind == "yt" else norm[("ln1", b)] + 1)
                    transposes(y, b * QT, QT, bank[7]).then_inc(misc_ps, 1)
                elif kind == "rt":
                    b = item[1]
                    pe.wait_ge(in_small, 16 * 8)
                    for t in range(QT):
                        last = mm(bank[7][:, t * E:(t + 1) * E], yT[:, (b * QT + t) * P:(b * QT + t + 1) * P], wr[:, :])
                    last.then_inc(misc_ps, 1)
                elif kind == "wt":
                    b = item[1]
                    pe.wait_ge(rt_w, b + 1)
                    for t in range(QT):
                        last = nc.tensor.transpose(bank[7][0:E, t * P:(t + 1) * P], wgt[:, b * QT + t, :], ident[:, :])
                    last.then_inc(misc_ps, 1)
                elif kind == "b2":
                    b = item[1]
                    for t in range(QT):
                        last = mm(bank[7][:, t * D:(t + 1) * D], wT[:, (b * QT + t) * P:(b * QT + t + 1) * P], b2[:, :])
                    last.then_inc(misc_ps, 1)
                elif kind == "hid":
                    n = item[1]
                    b, e = n // E, n % E
                    if n == 0:
                        pe.wait_ge(st_exp, UNITS)
                        pe.wait_ge(in_w1, 16)
                    if n % E == 0:
                        pe.wait_ge(misc_done, misc[("yt", b)])
                    for f in range(FT):
                        if n >= 1:
                            pe.wait_ge(h_sb, (n - 1) * FT + f + 1)
                        mm(bank[f][:, 0:S], w1[:, e, f * P:(f + 1) * P], yT[:, b * S:(b + 1) * S]).then_inc(h_ps, 1)
                elif kind == "yy":
                    n = item[1]
                    b, e = n // E, n % E
                    if n == 0:
                        pe.wait_ge(in_w2, 16)
                        pe.wait_ge(mx_done, UNITS * QT)
                    if n >= 2:
                        pe.wait_ge(y_acc, n - 1)
                    pe.wait_ge(h_sb, FT * (n + 1))
                    for t in range(QT):
                        for f in range(FT):
                            last = mm(bank[4 + n % 2][:, t * D:(t + 1) * D], hT[:, n % 2, f, t * P:(t + 1) * P],
                                      w2[:, e, f, :], start=(f == 0), stop=(f == FT - 1))
                    last.then_inc(y_ps, 1)
                elif kind == "kp":
                    n = item[1]
                    b, g = n // G, n % G
                    if n == 0:
                        pe.wait_ge(in_wk, 16)
                        pe.wait_ge(o0_sb, B * G + 1)
                    else:
                        pe.wait_ge(rot_m, n)
                    for part in range(2):
                        last = mm(bank[6 + part], wk1[:, 2 * g + part, :], ctxT[:, b * S2:(b + 1) * S2])
                    last.then_inc(misc_ps, 1)
                elif kind == "q1":
                    _, b, i = item
                    if i == 0:
                        pe.wait_ge(misc_done, misc[("l1t", b)])
                        pe.wait_ge(in_wq, 16)
                    for p in range(2):
                        w = (2 * i + p) * P
                        last = mm(bank[7][:, p * S:(p + 1) * S], wq1[:, w:w + P], yT[:, b * S:(b + 1) * S])
                    last.then_inc(misc_ps, 1)
                elif kind == "s1":
                    u = item[1]
                    b, h = u // H, u % H
                    p, e = h // 2, h % 2
                    if h == 0:
                        pe.wait_ge(misc_done, misc[("q1", b, 3)])
                    if u == 0:
                        pe.wait_ge(h_sb, B * E * FT)
                    if h == 0:
                        for i in range(2):
                            pe.wait_ge(rkey_out[i], 16 * 8 * (b + 1) * G // 2)
                    if u >= 2:
                        pe.wait_ge(st_exp, UNITS + u - 1)
                    for k in range(KT):
                        last = mm(st2[u % 2][:, k * S:(k + 1) * S], kT1[64 * e:64 * e + 64, b, p, k * P:(k + 1) * P],
                                  qT1[64 * e:64 * e + 64, b, p, :])
                    last.then_inc(st_ps, 1)
                elif kind == "o1":
                    n = item[1]
                    b, p = n // PAIRS, n % PAIRS
                    pe.wait_ge(clipped, 2 * n + 2)
                    if n >= 2:
                        pe.wait_ge(o1_sb, n - 1)
                    elif n == 0:
                        pe.wait_ge(y_acc, B * E)
                    dst = bank[4 + n % 2]
                    for k in range(KT):
                        for e in range(2):
                            h = 2 * p + e
                            mm(dst[64 * e:64 * e + 64, 0:S], v1[:, b * KT + k, h * DK1:(h + 1) * DK1],
                               prob[:, (2 * n + e) % RING, k * S:(k + 1) * S], start=(k == 0), stop=(k == KT - 1))
                    pe.wait_ge(summed, 2 * n + 2)
                    for e in range(2):
                        last = mm(dst[64 * e:64 * e + 64, S:2 * S], ones[:, 0:64], sums[:, (2 * n + e) % 4, :])
                    last.then_inc(pv1, 1)
                elif kind == "w1o":
                    b = item[1]
                    if b == 0:
                        pe.wait_ge(in_wo, 16)
                        pe.wait_ge(sc_sb, 1)
                        mm(bank[6][:, 0:1], ones[:, :], sc[:, 1:2]).then_inc(sc_ps, 1)
                    pe.wait_ge(o1_sb, PAIRS * (b + 1))
                    for t in range(QT):
                        for p in range(PAIRS):
                            tok = (b * QT + t) * P
                            last = mm(bank[7][:, t * D:(t + 1) * D], oT1[:, p, tok:tok + P], wo1[:, p, :],
                                      start=(p == 0), stop=(p == PAIRS - 1))
                    last.then_inc(misc_ps, 1)

            pe.wait_ge(misc_done, len(misc))
            pe.wait_ge(sc_sb, 2)
            nc.tensor.transpose(bank[7][0:1, 0:P], sc[:, 0:1], ident[:, :]).then_inc(sc_ps, 1)
            pe.wait_ge(sc_sb, 3)
            mm(bank[7][:, 0:1], ones[0:1, :], sc[0:1, 1:2]).then_inc(sc_ps, 1)
            pe.wait_ge(qz_sb, 1)
            for t in range(TT):
                last = nc.tensor.transpose(bank[4].bitcast(bf16)[:, t * P:(t + 1) * P], qzb[:, t, :], identb[:, :])
            last.then_inc(qz_ps, 1)
            pe.wait_ge(qzT_sb, 1)
            for t in range(TT):
                last = mm(bank[6][:, t * D:(t + 1) * D], qzT[:, t * P:(t + 1) * P], qw[:, 0, :])
            last.then_inc(f_ps, 1)


def kernel(**inputs):
    import concourse.bacc as bacc
    from concourse.bass_utils import run_bass_kernel_spmd

    v = {n: np.asarray(a) for n, a in inputs.items()}
    dh = np.arange(D).reshape(H, DK0).T.reshape(-1)
    wkv = v["L1_xattn_Wkv"]
    wk = wkv[:, :H * DK1].reshape(D, G, 4, 2, 32).transpose(0, 1, 3, 2, 4).reshape(D, H * DK1)
    arrays = {
        "x": v["x"].reshape(TT, P, D),
        "ctx": v["ctx_1024"].reshape(CT, P, D),
        "ctxT": v["ctx_1024"].reshape(C, D).T,
        "mask": v["mask_BxS2_bf1"].reshape(1, C).view(np.uint8),
        "l0w": np.stack([v["L0_xattn_Wq"].T[:, dh], v["L0_xattn_Wk"].T[:, dh], v["L0_xattn_Wv"].T, v["L0_xattn_Wo"].T]),
        "bias0": v["L0_xattn_bo"].reshape(1, D),
        "bias1": v["L1_xattn_bo"].reshape(1, D),
        "bias2": v["L1_ffn_bias"].reshape(1, D),
        "brow": v["L0_ffn_b_router"].reshape(1, E),
        "lncol": np.stack([v["L1_xattn_ln_lat_g"], v["L1_xattn_ln_lat_b"], v["L1_xattn_ln_ctx_g"], v["L1_xattn_ln_ctx_b"]], axis=1),
        "wr": v["L0_ffn_W_router"], "w1": v["L0_ffn_W1"], "b1": v["L0_ffn_b1"].reshape(E, FT, P).transpose(2, 0, 1), "w2": v["L0_ffn_W2"], "b2": v["L0_ffn_b2"],
        "cosT": v["L1_xattn_cos"].T, "sinT": v["L1_xattn_sin"].T,
        "wq1": v["L1_xattn_Wq"], "wk1": wk, "wv1": wkv[:, H * DK1:], "wo1": v["L1_xattn_Wo"],
        "wf": v["L1_ffn_weight"].T,
    }
    arrays = {n: np.ascontiguousarray(a) for n, a in arrays.items()}
    nc = bacc.Bacc("TRN2", target_bir_lowering=False, num_devices=1)
    aps = {n: nc.dram_tensor("in_" + n, a.shape, mybir.dt.from_np(a.dtype), kind="ExternalInput").ap()
           for n, a in arrays.items()}
    out = nc.dram_tensor("out_0", (TT, P, D), mybir.dt.float32, kind="ExternalOutput").ap()
    build(nc, aps, out)
    r = run_bass_kernel_spmd(nc, [{"in_" + n: a for n, a in arrays.items()}], core_ids=[0])
    return r.results[0]["out_0"].reshape(B, S, D)
```

```python
import math
from contextlib import ExitStack

import numpy as np

import concourse.bass as bass
from concourse import mybir

P = 128
B, S, S2, D = 2, 256, 512, 128
T, C = B * S, B * S2
TT, CT = T // P, C // P
QT, KT = S // P, S2 // P
H = 16
DK0 = D // H
DK1 = 64
HALF = DK1 // 2
PAIRS = H // 2
G = H // 4
E, FF, FT = 8, 4 * D, 4
NPART = 3
ROWS = NPART * NPART * DK0
MASK_ROW = ROWS
MAX_ROW = 96
NEG = 1.0e10
EPS = 1e-5
CLIP = 11.0
RING = 8
RING1 = 6
EARLY = 4
UNITS = B * H
ONE_ONE = float(np.uint32(0x3F803F80).view(np.float32))
MAGIC = 1.5 * 2.0 ** 23


def build(nc, a, out):
    f32, f32r, bf16, u8 = mybir.dt.float32, mybir.dt.float32r, mybir.dt.bfloat16, mybir.dt.uint8
    ALU, ACT, AX = mybir.AluOpType, mybir.ActivationFunctionType, mybir.AxisListType

    ctx = ExitStack()
    with ctx:
        def sb(name, shape, dt=f32):
            return ctx.enter_context(nc.sbuf_tensor(name, shape, dt))

        def over(name, shape, dt, offset):
            return nc.alloc_sbuf_tensor_at(name, shape, dt, offset=offset)

        def next_at():
            return (nc.sbuf_base + 31) // 32 * 32

        def sem(name):
            return ctx.enter_context(nc.semaphore(name))

        k_scr = nc.dram_tensor("k_scr", (B, NPART, P, S2), bf16, kind="Internal").ap()
        q_scr = nc.dram_tensor("q_scr", (B, NPART, P, S), bf16, kind="Internal").ap()
        m_scr = nc.dram_tensor("m_scr", (NPART, C), bf16, kind="Internal").ap()

        reg_k_at = next_at()
        reg_k = sb("reg_k", [P, 8192])
        Ks = reg_k[:, :].bitcast(bf16).rearrange("p (b h t) -> p b h t", b=B, h=H)
        kst0 = over("kst0", [P, H, S2], f32r, reg_k_at)
        reg_q = sb("reg_q", [P, 4096])
        Qs = reg_q[:, :].bitcast(bf16).rearrange("p (b h t) -> p b h t", b=B, h=H)
        rk1 = reg_q[:, :].rearrange("p (g h t) -> p g h t", g=G, h=2)
        wo1 = reg_q[:, 0:PAIRS * D].rearrange("p (a d) -> p a d", a=PAIRS)
        reg_p = sb("reg_p", [P, RING * 1024])
        prob = reg_p[:, :].rearrange("p (r n) -> p r n", r=RING)
        rot = reg_p[:, :].rearrange("p (r h w n) -> p r h w n", r=G, h=2, w=2)
        kround = reg_p[:, 6144:8192].rearrange("p (r n) -> p r n", r=4)
        qz = reg_p[:, 0:512].rearrange("p (t d) -> p t d", t=TT)
        qzb = reg_p[:, 512:768].bitcast(bf16).rearrange("p (t d) -> p t d", t=TT)
        qzT = reg_p[:, 768:1024].bitcast(bf16)
        reg_z = sb("reg_z", [P, 4096])
        kf = reg_z[:, 0:1024]
        qf = reg_z[:, 1024:1536]
        res = reg_z[:, 1536:2048]
        res2 = res[:, 0:S]
        kparts = reg_z[:, 2048:2048 + 768].bitcast(bf16).rearrange("p (j t) -> p j t", j=NPART)
        qparts = reg_z[:, 2816:2816 + 384].bitcast(bf16).rearrange("p (j t) -> p j t", j=NPART)
        kparts1 = reg_z[:, 3200:3200 + 768].bitcast(bf16).rearrange("p (j t) -> p j t", j=NPART)
        reg_y = sb("reg_y", [P, 384])
        qparts1 = reg_y[:, :].bitcast(bf16).rearrange("p (j t) -> p j t", j=NPART)
        o0 = reg_z[:, 0:2048].rearrange("p (g q) -> p g q", g=B * G)
        hT = reg_z[:, 2048:4096].rearrange("p (r f t) -> p r f t", r=2, f=FT)
        oT1 = reg_z[:, :].rearrange("p (b a t) -> p b a t", b=B, a=PAIRS)
        w1_at = next_at()
        w1 = sb("w1", [P, E, FF])
        w2_at = next_at()
        w2 = sb("w2", [P, E, FT, D])
        wv1 = reg_p[:, 7168:8192]
        kst1 = [over(f"kst1_{i}", [P, H // 2, S2], f32r, at) for i, at in enumerate((w1_at, w2_at))]
        v1 = sb("v1", [P, CT, H * DK1])
        v0 = sb("v0", [P, CT, H, DK0 + 1])
        ctx_tok = sb("ctx_tok", [P, CT, D])
        wq1 = ctx_tok[:, :, :].rearrange("p c d -> p (c d)")
        ctxT = sb("ctxT", [P, C])
        x = sb("x", [P, TT, D])
        xb = sb("xb", [P, TT, D])
        y = sb("y", [P, TT, D])
        yT = sb("yT", [P, T])
        l0w = sb("l0w", [P, 4, D])
        wk1_at = next_at()
        wk1 = sb("wk1", [P, 2 * G, P])
        sums = ctxT[:, :].rearrange("p (r q) -> p r q", r=4)
        half_sums = v0[:, :, :, :].rearrange("p c h d -> p (c h d)")[:, 0:2 * S].rearrange("p (k q) -> p k q", k=2)
        reg_r_at = next_at()
        reg_r = sb("reg_r", [P, 2 * S2])
        cosT, sinT = reg_r[:, 0:S2], reg_r[:, S2:2 * S2]
        qq = [over(f"qq{i}", [P, 2, 2 * S], f32r, at) for i, at in enumerate((wk1_at, reg_r_at))]
        maskb = sb("maskb", [P, C], u8)
        mask16 = sb("mask16", [16, C // 16], u8)
        mval = sb("mval", [16, 2, C // 16])
        mpart = sb("mpart", [16, NPART, C // 16], bf16)
        bias0, bias1, bias2 = (sb(n, [P, D]) for n in ("bias0", "bias1", "bias2"))
        lncol = sb("lncol", [P, 4])
        wr = sb("wr", [P, E])
        brow = sb("brow", [P, E])
        b1 = sb("b1", [P, E, FT])
        b2 = sb("b2", [E, D])
        wf = sb("wf", [P, D])
        ident = sb("ident", [P, P])
        identb = sb("identb", [P, P], bf16)
        ones = sb("ones", [P, P])
        tri = sb("tri", [P, E, E])
        mhalf = sb("mhalf", [P, 1])
        onesb = sb("onesb", [NPART, P], bf16)
        done_col = sb("done_col", [P, 1])
        st = sb("st", [P, CT + TT, 6])
        mv = sb("mv", [P, CT + TT, 2])
        ve = sb("ve", [P, CT + TT])
        rstd = sb("rstd", [P, CT + TT])
        shift = sb("shift", [P, CT])
        nmax = sb("nmax", [P, 2 * B, QT * H // 2])
        maxres = sb("maxres", [H, P])
        maxpart = sb("maxpart", [H, 2 * B, NPART, P], bf16)
        rs0 = sb("rs0", [P, TT, H])
        rs1 = sb("rs1", [P, 2, S])
        on0 = rs1[:, :, :].rearrange("p r (h d) -> p (r h) d", h=2 * H).rearrange("p (t h) d -> p t h d", t=TT)
        wT = rs1[0:E, :, :].rearrange("p r q -> p (r q)")
        oT0 = yT
        gt = sb("gt", [P, QT, E, E])
        eq = sb("eq", [P, QT, E, E])
        lg = sb("lg", [P, TT, E])
        rank = sb("rank", [P, TT, E])
        top = sb("top", [P, TT])
        ex = sb("ex", [P, TT, E])
        wgt = sb("wgt", [P, TT, E])
        qw = sb("qw", [P, 2, D], bf16)
        sc = sb("sc", [P, 8])

        st2 = [ctx.enter_context(nc.psum_tensor(f"st{i}", [P, 1024], f32)) for i in range(2)]
        b4, b5, b6, b7 = (ctx.enter_context(nc.psum_tensor(f"b{i}", [P, 512], f32)) for i in (4, 5, 6, 7))
        bank = [st2[0][:, 0:512], st2[0][:, 512:1024], st2[1][:, 0:512], st2[1][:, 512:1024],
                b4[:, :], b5[:, :], b6[:, :], b7[:, :]]

        in_x, in_w0, in_ctxT, in_mask, in_ctx, in_cols, in_wv, in_rope, in_wk, in_small, in_w1, in_w2, \
            in_wq, in_wo = (sem("in_" + n) for n in (
                "x", "w0", "ctxT", "mask", "ctx", "cols", "wv", "rope", "wk", "small", "w1", "w2", "wq", "wo"))
        consts = sem("consts")
        pool_step = sem("pool_step")
        stats = sem("stats")
        pow_done = sem("pow_done")
        dve_step = sem("dve_step")
        normed = sem("normed")
        tr = sem("tr")
        k0_ps, q0_ps, v0_ps = sem("k0_ps"), sem("q0_ps"), sem("v0_ps")
        q0_f, v0_sb = sem("q0_f"), sem("v0_sb")
        parts = sem("parts")
        mparts = sem("mparts")
        scr_k, scr_q = sem("scr_k"), sem("scr_q")
        scr_m = sem("scr_m")
        stack = [sem(f"stack{b}") for b in range(B)]
        ctx_shift, ctx_normed = sem("ctx_shift"), sem("ctx_normed")
        ctxn = sem("ctxn")
        v1_ps, v1_sb = sem("v1_ps"), sem("v1_sb")
        mx_ps, mx_done = sem("mx_ps"), sem("mx_done")
        misc_ps, misc_done = sem("misc_ps"), sem("misc_done")
        mt_parts = sem("mt_parts")
        max_rows = [sem(f"max_rows{q}") for q in range(2 * B)]
        st_ps, st_exp = sem("st_ps"), sem("st_exp")
        clipped, summed = sem("clipped"), sem("summed")
        pv0, o0_sb = sem("pv0"), sem("o0_sb")
        yT_sb = sem("yT_sb")
        rt_lg, rt_ex, rt_w = sem("rt_lg"), sem("rt_ex"), sem("rt_w")
        h_ps, h_sb, y_ps, y_acc = sem("h_ps"), sem("h_sb"), sem("y_ps"), sem("y_acc")
        rot_m, rkey_sb = sem("rot_m"), sem("rkey_sb")
        kh_sb, kl_sb = sem("kh_sb"), sem("kl_sb")
        kst_out = [[sem(f"kst{b}_out{i}") for i in range(2)] for b in range(B)]
        xbias, x_new = sem("xbias"), sem("x_new")
        q1_ps, qh_sb, ql_sb = sem("q1_ps"), sem("qh_sb"), sem("ql_sb")
        pv1, o1_sb = sem("pv1"), sem("o1_sb")
        sc_ps, sc_sb = sem("sc_ps"), sem("sc_sb")
        qz_sb, qz_ps, qzT_sb, f_ps, fin = (sem(n) for n in ("qz_sb", "qz_ps", "qzT_sb", "f_ps", "fin"))
        stored = sem("stored")

        block = ctx.enter_context(nc.Block())

        order = []
        maxima = [("mx", q, i) for q in range(2 * B) for i in range(H)]

        def next_maxima(n):
            for _ in range(min(n, len(maxima))):
                order.append(maxima.pop(0))
                if order[-1][2] == 1 and order[-1][1]:
                    order.append(("mt", order[-1][1] - 1))
            if order[-1][0] == "st" and ("mt", 2 * B - 1) not in order:
                order.append(("mt", 2 * B - 1))

        for n in range(EARLY, 2 * CT):
            next_maxima(2)
            order.append(("v1", n))
        next_maxima(3 * H // 2 + 2 - 2 * (2 * CT - EARLY))
        tail = [[("t1", b * QT), ("t1", b * QT + 1), ("t2", b), ("wo", b), ("yt", b), ("rt", b), ("wt", b), ("b2", b)]
                for b in range(B)]
        tail_at = dict(zip((20, 21, 22, 24, 27, 29), tail[0]))
        for u in range(UNITS):
            order.append(("st", u))
            next_maxima(1)
            if u > 4 and u % 4:
                order.append(("pv", u // 4 - 1, u % 4 - 1))
            next_maxima(1)
            if u > 4 and u % 4 == 3:
                order.append(("pv", u // 4 - 1, 3))
            if u in tail_at:
                order.append(tail_at[u])
        order += [("pv", 2 * G - 1, k) for k in range(KT)]
        order += [("hid", 0), ("wt", 0)]
        left = list(tail[1])
        kp_at = {1: 0, 2: 1, 4: 2, 6: 3, 9: 4, 10: 5, 11: 6, 12: 7}
        for n in range(B * E):
            if n + 1 < B * E:
                order.append(("hid", n + 1))
            if n == 0:
                order.append(("b2", 0))
            if n in kp_at:
                order.append(("kp", kp_at[n]))
            order.append(("yy", n))
            if kp_at.get(n - 1, G) < G:
                order.append(("ks", kp_at[n - 1]))
            if n < E:
                order.append(left.pop(0))
            if E - 1 <= n < E + 2:
                order.append(("ln1", 0, n - E + 1))
            if n == E + 2:
                order.append(("l1t", 0))
            if n >= B * E - 2:
                order.append(("q1", n - B * E + 2))
        for n in range(UNITS // 2):
            for e in range(2):
                order.append(("s1", 2 * n + e))
                if n == 0 and e == 0:
                    order.append(("ln1", 1, 0))
            if n + 2 < UNITS // 2:
                order.append(("q1", n + 2))
            if n < 2:
                order.append(("ln1", 1, n + 1))
            if n:
                order.append(("o1", n - 1))
            if n < G:
                order.append(("ks", G + n))
            if n == 2:
                order.append(("l1t", 1))
            if n == PAIRS + 2:
                order.append(("w1o", 0))
        order += [("w1p", 0, 3), ("o1", UNITS // 2 - 1), ("w1p", 3, PAIRS - 1), ("w1o", 1)]
        misc = {}
        norm = {}
        for item in order:
            if item[0] in ("mt", "t1", "t2", "wo", "yt", "rt", "wt", "b2", "kp", "l1t", "w1o"):
                misc[item] = len(misc) + 1
            if item[0] in ("wo", "w1o") or item[0] == "ln1" and item[2]:
                norm[item] = 2 + len(norm)

        def key_parts(i):
            if i < G:
                return rot[:, i, :, 1, :], rot[:, i, :, 0, :]
            i -= G
            return kround[:, 2 * (i % 2):2 * (i % 2) + 2, :], rk1[:, i // 2 * 2:i // 2 * 2 + 2, i % 2, :]

        def stacked(b, h):
            return kst0[:, h, :] if b == 0 else kst1[h // (H // 2)][:, h % (H // 2), :]

        def stacked_half(b, g, j, part, half):
            r = part * DK1 + half * HALF
            if b == 0:
                return kst0[r:r + HALF, 4 * g + j:4 * g + j + 5:4, :].bitcast(f32)
            return kst1[g // 2][r:r + HALF, j:j + 5:4, :].bitcast(f32)

        @block.sync
        def _(sp):
            def load(dst, src, s):
                sp.dma_start(dst, src).then_inc(s, 16)

            load(x[:, :, :], a["x"].rearrange("t p d -> p t d"), in_x)
            load(ctxT[:, :], a["ctxT"], in_ctxT)
            load(l0w[:, :, :], a["l0w"].rearrange("n p d -> p n d"), in_w0)
            load(mask16[:, :], a["mask"].rearrange("a (p n) -> (a p) n", p=16), in_mask)
            load(maskb[:, :], a["mask"].broadcast_to([P, C]), in_mask)
            load(ctx_tok[:, :, :], a["ctx"].rearrange("t p d -> p t d"), in_ctx)
            load(wv1, a["wv1"], in_wv)
            for dst, name in ((bias0, "bias0"), (bias1, "bias1"), (bias2, "bias2"), (brow, "brow")):
                load(dst[:, :], a[name].broadcast_to([P, dst.shape[1]]), in_small)
            load(wr[:, :], a["wr"], in_small)
            load(b1[:, :, :], a["b1"], in_small)
            load(b2[:, :], a["b2"], in_small)
            load(wf[:, :], a["wf"], in_small)
            for b in range(B):
                kp = kparts if b == 0 else kparts1
                qp = qparts if b == 0 else qparts1

                def stack_keys(i):
                    r = i * NPART * DK0
                    sp.dma_start(Ks[r:r + NPART * DK0, b, :, :],
                                 k_scr[b].rearrange("j (d h) t -> (j d) h t", h=H)).then_inc(stack[b], 16)

                def stack_queries(i):
                    r = i * NPART * DK0
                    sp.dma_start(Qs[r:r + NPART * DK0, b, :, :].rearrange("p h t -> p (h t)"),
                                 q_scr[b, i].rearrange("(d h) t -> d (h t)", h=H)[None, :, :]
                                 .broadcast_to([NPART, DK0, H * S])).then_inc(stack[b], 16)

                sp.wait_ge(parts, 2 * b + 1)
                sp.dma_start(k_scr[b].rearrange("j p t -> p j t"), kp).then_inc(scr_k, 16)
                if b == 0:
                    sp.wait_ge(mparts, 1)
                    sp.dma_start(m_scr.rearrange("j (p n) -> p j n", p=16), mpart[:, :, :]).then_inc(scr_m, 16)
                sp.wait_ge(parts, 2 * b + 2)
                sp.dma_start(q_scr[b].rearrange("j p t -> p j t"), qp).then_inc(scr_q, 16)
                sp.wait_ge(scr_k, 16 * (b + 1))
                for i in range(NPART - 1):
                    stack_keys(i)
                sp.wait_ge(scr_q, 16 * (b + 1))
                for i in range(NPART - 1):
                    stack_queries(i)
                sp.wait_ge(consts, b + 2)
                stack_keys(NPART - 1)
                stack_queries(NPART - 1)
                sp.dma_start(Ks[MAX_ROW:MAX_ROW + NPART, b, :, :].rearrange("j h (k n) -> j (h k) n", n=P),
                             onesb[:, None, :].broadcast_to([NPART, H * KT, P])).then_inc(stack[b], 16)
                if b == 0:
                    sp.wait_ge(scr_m, 16)
                sp.dma_start(Ks[MASK_ROW:MASK_ROW + NPART, b, :, :],
                             m_scr[:, None, b * S2:(b + 1) * S2].broadcast_to([NPART, H, S2])).then_inc(stack[b], 16)
            for q in range(4):
                load(cosT[32 * q:32 * q + 32, :], a["cosT"], in_rope)
                load(sinT[32 * q:32 * q + 32, :], a["sinT"], in_rope)
            load(wk1[:, :, :], a["wk1"].rearrange("p (n c) -> p n c", n=2 * G), in_wk)
            for q in range(2 * B):
                b, h0 = q // 2, 8 * (q % 2)
                sp.wait_ge(mt_parts, q + 1)
                for j in range(NPART):
                    sp.dma_start(Qs[MAX_ROW + j:MAX_ROW + j + 1, b, h0:h0 + 8, :].rearrange("j h (t n) -> j (h t) n", t=QT),
                                 maxpart[:, q, j, :]).then_inc(max_rows[q], 16)
                if q == 0:
                    load(w1[:, :, :], a["w1"].rearrange("e p f -> p e f"), in_w1)
                elif q == 1:
                    load(w2[:, :, :, :], a["w2"].rearrange("e (f p) d -> p e f d", p=P), in_w2)
            sp.wait_ge(tr, 3)
            sp.dma_start(wq1, a["wq1"]).then_inc(in_wq, 16)
            sp.wait_ge(st_ps, UNITS)
            for i in range(G // 2):
                sp.wait_ge(kl_sb, 2 * i + 2)
                for half in range(2):
                    for part in range(2):
                        for j in range(4):
                            sp.dma_start(stacked_half(0, 2 * i, j, part, half),
                                         rot[HALF * j:HALF * (j + 1), 2 * i:2 * i + 2, half, 1 - part, :]
                                         ).then_inc(kst_out[0][i], 16)
            sp.wait_ge(h_ps, B * E * FT)
            sp.wait_ge(y_ps, B * E)
            for i in range(G):
                sp.wait_ge(kl_sb, G + i + 1)
                for part in range(2):
                    for j in range(4):
                        sp.dma_start(stacked_half(1, i // 2 * 2, j, part, i % 2),
                                     key_parts(G + i)[part][HALF * j:HALF * (j + 1), :, :]).then_inc(kst_out[1][i % 2], 16)
            for i in range(2):
                sp.wait_ge(kst_out[1][i], 16 * 8)
            sp.dma_start(wo1, a["wo1"].rearrange("(a p) d -> p a d", p=P)).then_inc(in_wo, 16)
            sp.wait_ge(fin, 1)
            sp.dma_start(out.rearrange("t p d -> p t d"), qz[:, :, :]).then_inc(stored, 16)
            sp.wait_ge(stored, 16)

        @block.gpsimd
        def _(pool):
            steps = [0]

            def link(ins):
                steps[0] += 1
                ins.then_inc(pool_step, 1)
                pool.wait_ge(pool_step, steps[0])

            nc.gpsimd.memset(mhalf[:, :], -0.5)
            nc.gpsimd.memset(ones[:, :], 1.0)
            nc.gpsimd.memset(onesb[:, :], 1.0)
            nc.gpsimd.memset(tri[:, :, :], 1.0)
            link(nc.gpsimd.memset(ident[:, :], 0.0))
            link(nc.gpsimd.affine_select(out=ident[:, :], in_=ident[:, :], compare_op=ALU.not_equal, fill=1.0,
                                         base=0, pattern=[[-1, P]], channel_multiplier=1))
            link(nc.gpsimd.tensor_copy(identb[:, :], ident[:, :]))
            nc.gpsimd.affine_select(out=tri[:, :, :], in_=tri[:, :, :], compare_op=ALU.is_ge, fill=0.0,
                                    base=-1, pattern=[[1, E], [-1, E]], channel_multiplier=0).then_inc(consts, 1)
            pool.wait_ge(consts, 1)
            powers = [0]

            def power(tiles, first=CT):
                powers[0] += 1
                pool.wait_ge(stats, powers[0])
                nc.gpsimd.tensor_tensor(rstd[:, first:first + tiles], ve[:, first:first + tiles],
                                        mhalf[:, :].broadcast_to([P, tiles]), ALU.pow).then_inc(pow_done, 1)

            link(nc.gpsimd.memset(reg_q[64:128, 0:2048], ONE_ONE))
            power(TT)
            pool.wait_ge(pow_done, 1)
            nc.gpsimd.memset(reg_k[64:128, 0:4096], 0.0).then_inc(consts, 1)
            pool.wait_ge(consts, 2)
            power(CT, 0)
            pool.wait_ge(pow_done, 2)
            pool.wait_ge(in_mask, 32)
            link(nc.gpsimd.tensor_scalar(mval[:, 0, :], mask16[:, :], NEG, NEG, ALU.mult, ALU.subtract))
            link(nc.gpsimd.tensor_copy(mpart[:, 0, :], mval[:, 0, :]))
            link(nc.gpsimd.tensor_tensor(mval[:, 1, :], mval[:, 0, :], mpart[:, 0, :], ALU.subtract))
            link(nc.gpsimd.tensor_copy(mpart[:, 1, :], mval[:, 1, :]))
            nc.gpsimd.tensor_tensor(mpart[:, 2, :], mval[:, 1, :], mpart[:, 1, :], ALU.subtract).then_inc(mparts, 1)
            pool.wait_ge(mparts, 1)
            link(nc.gpsimd.memset(v0[:, :, :, DK0:DK0 + 1], 1.0))
            link(nc.gpsimd.memset(reg_q[64:128, 2048:4096], ONE_ONE))
            nc.gpsimd.memset(reg_k[64:128, 4096:8192], 0.0).then_inc(consts, 1)
            pool.wait_ge(consts, 3)
            pool.wait_ge(in_small, 16 * 8)
            nc.gpsimd.tensor_tensor(xb[:, :, :], x[:, :, :], bias0[:, None, :].broadcast_to([P, TT, D]),
                                    ALU.add).then_inc(xbias, 1)
            for item in order:
                kind = item[0]
                if kind == "mt":
                    pool.wait_ge(misc_done, misc[item])
                    dst = maxpart[:, item[1], :, :]
                    link(nc.gpsimd.tensor_copy(dst[:, 1, :], maxres[:, :]))
                    nc.gpsimd.tensor_tensor(dst[:, 2, :], maxres[:, :], dst[:, 1, :], ALU.subtract).then_inc(mt_parts, 1)
                    pool.wait_ge(mt_parts, item[1] + 1)
                elif kind == "wo":
                    power(QT)
                elif kind == "ln1":
                    _, b, i = item
                    if i < 2:
                        power(QT)
                    if i != 1:
                        continue
                    pool.wait_ge(x_new, B + b + 1)
                    nc.gpsimd.tensor_tensor(xb[:, b * QT:(b + 1) * QT, :], x[:, b * QT:(b + 1) * QT, :],
                                            bias1[:, None, :].broadcast_to([P, QT, D]), ALU.add).then_inc(xbias, 1)
                elif kind == "kp":
                    n = item[1]
                    pool.wait_ge(rot_m, n + 1)
                    for half, op in ((0, ALU.subtract), (1, ALU.add)):
                        src = rot[:, n % G, half, :, :]
                        dst = src[:, 0, :] if n < G else rk1[:, n - G, half, :]
                        nc.gpsimd.tensor_tensor(dst, src[:, 0, :], src[:, 1, :], op).then_inc(rkey_sb, 1)
                elif kind == "s1":
                    u = item[1]
                    pool.wait_ge(clipped, u + 1)
                    if u:
                        pool.wait_ge(summed, u)
                    p4 = prob[:, u % RING1, :].rearrange("p (k q) -> p k q", k=KT)
                    link(nc.gpsimd.tensor_tensor(half_sums, p4[:, 0:2, :], p4[:, 2:4, :], ALU.add))
                    if u >= 4:
                        pool.wait_ge(pv1, (u - 4) // 2 + 1)
                    nc.gpsimd.tensor_tensor(sums[:, u % 4, :], half_sums[:, 0, :], half_sums[:, 1, :],
                                            ALU.add).then_inc(summed, 1)
                elif kind == "w1o":
                    b = item[1]
                    power(QT)
                    pool.wait_ge(x_new, 2 * B + b + 1)
                    nc.gpsimd.tensor_tensor(xb[:, b * QT:(b + 1) * QT, :], x[:, b * QT:(b + 1) * QT, :],
                                            bias2[:, None, :].broadcast_to([P, QT, D]), ALU.add).then_inc(xbias, 1)

        @block.scalar
        def _(act):
            def load(dst, src, s):
                act.dma_start(dst, src).then_inc(s, 16)

            load(lncol[:, :], a["lncol"], in_cols)

            def values(n):
                act.wait_ge(v1_ps, n + 1)
                nc.scalar.activation(v1[:, n // 2, 512 * (n % 2):512 * (n % 2) + 512], bank[n % 4],
                                     ACT.Copy).then_inc(v1_sb, 1)

            act.wait_ge(q0_ps, 1)
            nc.scalar.activation(qf, bank[6], ACT.Copy, scale=1.0 / math.sqrt(DK0)).then_inc(q0_f, 1)
            act.wait_ge(ctx_shift, 1)
            for c in range(CT):
                last = nc.scalar.activation(ctx_tok[:, c, :], ctx_tok[:, c, :], ACT.Identity, scale=rstd[:, c:c + 1],
                                            bias=shift[:, c:c + 1])
            last.then_inc(ctx_normed, 1)
            for i in range(2):
                act.wait_ge(v0_ps, i + 1)
                nc.scalar.activation(v0[:, 4 * i:4 * i + 4, :, 0:DK0],
                                     bank[2 + i].rearrange("p (c h d) -> p c h d", c=4, h=H),
                                     ACT.Copy).then_inc(v0_sb, 1)
            act.wait_ge(in_cols, 16)
            for i in range(2):
                act.wait_ge(tr, 2 + i)
                nc.scalar.activation(ctxT[:, 512 * i:512 * i + 512], bank[i], ACT.Identity,
                                     scale=lncol[:, 2:3], bias=lncol[:, 3:4]).then_inc(ctxn, 1)
            for n in range(EARLY):
                values(n)
            for item in order:
                kind = item[0]
                if kind == "v1":
                    values(item[1])
                elif kind == "st":
                    u = item[1]
                    act.wait_ge(st_ps, u + 1)
                    if u >= RING:
                        act.wait_ge(pv0, u // 4 - 1)
                    nc.scalar.activation(prob[:, u % RING, :], st2[u % 2][:, :], ACT.Exp).then_inc(st_exp, 1)
                elif kind == "pv" and item[2] == KT - 1:
                    g = item[1]
                    act.wait_ge(pv0, g + 1)
                    if g == 0:
                        act.wait_ge(stack[1], 16 * 8)
                    nc.scalar.activation(o0[:, g, :], bank[6][:, 0:S], ACT.Copy).then_inc(o0_sb, 1)
                elif kind == "rt":
                    b = item[1]
                    act.wait_ge(rt_lg, b + 1)
                    nc.scalar.activation(ex[:, b * QT:(b + 1) * QT, :], lg[:, b * QT:(b + 1) * QT, :],
                                         ACT.Exp).then_inc(rt_ex, 1)
                elif kind == "hid":
                    n = item[1]
                    for f in range(FT):
                        act.wait_ge(h_ps, n * FT + f + 1)
                        if n >= 2:
                            act.wait_ge(y_ps, n - 1)
                        nc.scalar.activation(hT[:, n % 2, f, :], bank[f][:, 0:S], ACT.Relu,
                                             bias=b1[:, n % E, f:f + 1]).then_inc(h_sb, 1)
                elif kind == "l1t":
                    b = item[1]
                    act.wait_ge(misc_ps, misc[item])
                    nc.scalar.activation(yT[:, b * S:(b + 1) * S], bank[7][:, 0:S], ACT.Identity,
                                         scale=lncol[:, 0:1], bias=lncol[:, 1:2]).then_inc(misc_done, 1)
                elif kind == "ks":
                    i = item[1]
                    act.wait_ge(rkey_sb, 2 * i + 2 if i < G else 2 * B * G)
                    if i >= G + 2:
                        act.wait_ge(kst_out[1][i % 2], 16 * 8)
                    rounded, rest = key_parts(i)
                    nc.scalar.activation(rounded.bitcast(f32r), rest, ACT.Copy).then_inc(kh_sb, 1)
                elif kind == "q1":
                    n = item[1]
                    act.wait_ge(q1_ps, n + 1)
                    if n >= 2:
                        act.wait_ge(st_ps, UNITS + 2 * n - 2)
                    nc.scalar.activation(qq[n % 2][:, 0, :], bank[6], ACT.Copy).then_inc(qh_sb, 1)
                elif kind == "s1":
                    u = item[1]
                    act.wait_ge(st_ps, UNITS + u + 1)
                    if u >= RING1:
                        act.wait_ge(pv1, (u - RING1) // 2 + 1)
                        act.wait_ge(summed, u - RING1 + 1)
                    elif u == 0:
                        act.wait_ge(rkey_sb, 2 * B * G)
                    nc.scalar.activation(prob[:, u % RING1, :], st2[u % 2][:, :], ACT.Exp,
                                         scale=DK1 ** -0.5).then_inc(st_exp, 1)

        @block.vector
        def _(dve):
            steps = [0]

            def link(ins):
                steps[0] += 1
                ins.then_inc(dve_step, 1)
                dve.wait_ge(dve_step, steps[0])

            norms = [0]

            def norm_stats(src, first, tiles, at=CT):
                for t in range(tiles):
                    last = nc.vector.bn_stats(st[:, at + t, :], src[:, first + t, :])
                link(last)
                for t in range(tiles):
                    last = nc.vector.bn_aggr(mv[:, at + t, :], st[:, at + t, :])
                link(last)
                nc.vector.tensor_scalar_add(ve[:, at:at + tiles], mv[:, at:at + tiles, 1], EPS).then_inc(stats, 1)
                norms[0] += 1

            def norm_apply(dst, src, first, tiles):
                dve.wait_ge(pow_done, norms[0])
                for t in range(tiles):
                    last = nc.vector.tensor_scalar(dst[:, first + t, :], src[:, first + t, :], mv[:, CT + t, 0:1],
                                                   rstd[:, CT + t:CT + t + 1], ALU.subtract, ALU.mult)
                last.then_inc(normed, 1)

            def layer_norm(dst, src, first, tiles):
                norm_stats(src, first, tiles)
                norm_apply(dst, src, first, tiles)

            def split(dst, src, tmp):
                link(nc.vector.tensor_copy(dst[0], src))
                link(nc.vector.tensor_tensor(tmp, src, dst[0], ALU.subtract))
                link(nc.vector.tensor_copy(dst[1], tmp))
                return nc.vector.tensor_tensor(dst[2], tmp, dst[1], ALU.subtract)

            def take(item):
                dve.wait_ge(misc_ps, misc[item])

            dve.wait_ge(in_x, 16)
            norm_stats(x, 0, TT)
            norm_apply(y, x, 0, TT)
            dve.wait_ge(in_ctx, 16)
            norm_stats(ctx_tok, 0, CT, at=0)
            dve.wait_ge(in_mask, 32)
            for b in range(B):
                kp = kparts if b == 0 else kparts1
                qp = qparts if b == 0 else qparts1
                dve.wait_ge(k0_ps, b + 1)
                link(nc.vector.tensor_tensor(kf[:, b * S2:(b + 1) * S2], bank[4 + b],
                                             maskb[:, b * S2:(b + 1) * S2], ALU.mult))
                if b == 0:
                    dve.wait_ge(tr, 1)
                    nc.vector.tensor_copy(yT[:, :], bank[7]).then_inc(yT_sb, 1)
                    dve.wait_ge(pow_done, 2)
                    nc.vector.scalar_tensor_tensor(out=shift[:, :], in0=mv[:, 0:CT, 0], scalar=-1.0, in1=rstd[:, 0:CT],
                                                   op0=ALU.mult, op1=ALU.mult).then_inc(ctx_shift, 1)
                split([kp[:, j, :] for j in range(NPART)], kf[:, b * S2:(b + 1) * S2], res).then_inc(parts, 1)
                if b == 0:
                    dve.wait_ge(q0_f, 1)
                dve.wait_ge(parts, 2 * b + 1)
                split([qp[:, j, :] for j in range(NPART)], qf[:, b * S:(b + 1) * S], res2).then_inc(parts, 1)
                dve.wait_ge(parts, 2 * b + 2)
            nc.vector.memset(bank[6], 0.0).then_inc(o0_sb, 1)

            mx = 0
            for item in order:
                kind = item[0]
                if kind == "mx":
                    _, q, i = item
                    mx += 1
                    dve.wait_ge(mx_ps, mx)
                    nc.vector.tensor_reduce(nmax[:, q, i:i + 1], bank[4 + mx % 2], AX.X, ALU.max,
                                            negate=True).then_inc(mx_done, 1)
                elif kind == "mt":
                    q = item[1]
                    take(item)
                    src = bank[7][0:H, 0:P]
                    dst = maxpart[:, q, :, :]
                    if q:
                        dve.wait_ge(mt_parts, q)
                    link(nc.vector.tensor_copy(dst[:, 0, :], src))
                    nc.vector.tensor_tensor(maxres[:, :], src, dst[:, 0, :], ALU.subtract).then_inc(misc_done, 1)
                elif kind == "t1":
                    t = item[1]
                    take(item)
                    o = bank[7].rearrange("p (h c) -> p h c", h=H)
                    link(nc.vector.reciprocal(rs0[:, t, :], o[:, :, DK0]))
                    nc.vector.tensor_tensor(on0[:, t, :, :], o[:, :, 0:DK0],
                                            rs0[:, t, :, None].broadcast_to([P, H, DK0]), ALU.mult).then_inc(misc_done, 1)
                elif kind == "t2":
                    b = item[1]
                    take(item)
                    nc.vector.tensor_copy(oT0[:, b * S:(b + 1) * S], bank[7][:, 0:S]).then_inc(misc_done, 1)
                elif kind in ("wo", "w1o"):
                    b = item[1]
                    dve.wait_ge(xbias, 1 if kind == "wo" else 1 + B)
                    take(item)
                    if item == ("w1o", 0):
                        nc.vector.tensor_scalar_mul(sc[:, 2:3], bank[7][:, S:S + 1], 1.0 / (D * D))
                    if item == ("w1o", 1):
                        for t in range(QT):
                            last = nc.vector.tensor_tensor(x[:, b * QT + t, :], bank[7 - t][:, 0:D], xb[:, b * QT + t, :],
                                                           ALU.add)
                        last.then_inc(misc_done, 1)
                    else:
                        nc.vector.tensor_tensor(x[:, b * QT:(b + 1) * QT, :],
                                                bank[7][:, 0:S].rearrange("p (t d) -> p t d", t=QT),
                                                xb[:, b * QT:(b + 1) * QT, :], ALU.add).then_inc(misc_done, 1)
                    dve.wait_ge(misc_done, misc[item])
                    nc.vector.tensor_copy(done_col[:, :], x[:, b * QT, 0:1]).then_inc(x_new, 1)
                    layer_norm(y, x, b * QT, QT)
                    if kind == "w1o":
                        dve.wait_ge(normed, norm[item])
                        nc.vector.tensor_reduce(sc[:, 3 * b:3 * b + 1], y[:, b * QT:(b + 1) * QT, :], AX.XY, ALU.max,
                                                apply_absolute_value=True).then_inc(sc_sb, 1)
                elif kind == "yt":
                    b = item[1]
                    take(item)
                    nc.vector.tensor_copy(yT[:, b * S:(b + 1) * S], bank[7][:, 0:S]).then_inc(misc_done, 1)
                elif kind == "rt":
                    b = item[1]
                    r = slice(b * QT, (b + 1) * QT)
                    take(item)
                    nc.vector.tensor_tensor(lg[:, r, :], bank[7][:, 0:QT * E].rearrange("p (t e) -> p t e", t=QT),
                                            brow[:, None, :].broadcast_to([P, QT, E]), ALU.add).then_inc(misc_done, 1)
                    dve.wait_ge(misc_done, misc[item])
                    nc.vector.tensor_reduce(top[:, r], lg[:, r, :], AX.X, ALU.max)
                    for t in range(QT):
                        lj = lg[:, b * QT + t, None, :].broadcast_to([P, E, E])
                        le = lg[:, b * QT + t, :, None].broadcast_to([P, E, E])
                        nc.vector.tensor_tensor(gt[:, t, :, :], lj, le, ALU.is_gt)
                        last = nc.vector.tensor_tensor(eq[:, t, :, :], lj, le, ALU.is_equal)
                    link(last)
                    nc.vector.tensor_tensor(lg[:, r, :], lg[:, r, :], top[:, r, None].broadcast_to([P, QT, E]),
                                            ALU.subtract).then_inc(rt_lg, 1)
                    link(nc.vector.tensor_tensor(eq[:, :, :, :], eq[:, :, :, :],
                                                 tri[:, None, :, :].broadcast_to([P, QT, E, E]), ALU.mult))
                    link(nc.vector.tensor_tensor(gt[:, :, :, :], gt[:, :, :, :], eq[:, :, :, :], ALU.add))
                    link(nc.vector.tensor_reduce(rank[:, r, :], gt[:, :, :, :], AX.X, ALU.add))
                    dve.wait_ge(rt_ex, b + 1)
                    link(nc.vector.scalar_tensor_tensor(out=wgt[:, r, :], in0=rank[:, r, :], scalar=2.0, in1=ex[:, r, :],
                                                        op0=ALU.is_lt, op1=ALU.mult))
                    link(nc.vector.tensor_reduce(top[:, r], wgt[:, r, :], AX.X, ALU.add))
                    link(nc.vector.reciprocal(top[:, r], top[:, r]))
                    nc.vector.tensor_tensor(wgt[:, r, :], wgt[:, r, :], top[:, r, None].broadcast_to([P, QT, E]),
                                            ALU.mult).then_inc(rt_w, 1)
                elif kind == "wt":
                    b = item[1]
                    take(item)
                    nc.vector.tensor_copy(wT[:, b * S:(b + 1) * S], bank[7][0:E, 0:S]).then_inc(misc_done, 1)
                elif kind == "b2":
                    b = item[1]
                    take(item)
                    nc.vector.tensor_tensor(x[:, b * QT:(b + 1) * QT, :], bank[7][:, 0:S].rearrange("p (t d) -> p t d", t=QT),
                                            x[:, b * QT:(b + 1) * QT, :], ALU.add).then_inc(misc_done, 1)
                    dve.wait_ge(misc_done, misc[item])
                elif kind == "yy":
                    n = item[1]
                    b, e = n // E, n % E
                    dve.wait_ge(y_ps, n + 1)
                    if n:
                        dve.wait_ge(y_acc, n)
                    for t in range(QT):
                        last = nc.vector.scalar_tensor_tensor(
                            out=x[:, b * QT + t, :], in0=bank[4 + n % 2][:, t * D:(t + 1) * D],
                            scalar=wgt[:, b * QT + t, e:e + 1], in1=x[:, b * QT + t, :], op0=ALU.mult, op1=ALU.add)
                    last.then_inc(y_acc, 1)
                    if e == E - 1:
                        dve.wait_ge(y_acc, n + 1)
                        nc.vector.tensor_copy(done_col[:, :], x[:, b * QT, 0:1]).then_inc(x_new, 1)
                elif kind == "kp":
                    n = item[1]
                    if n == 0:
                        dve.wait_ge(in_rope, 16 * 8)
                    if n >= G:
                        dve.wait_ge(kst_out[0][(n - G) // 2], 16 * 16)
                    r = rot[:, n % G, :, :, :]
                    take(item)
                    nc.vector.tensor_tensor(r[:, 0, 1, :], bank[7], sinT, ALU.mult)
                    nc.vector.tensor_tensor(r[:, 1, 0, :], bank[7], cosT, ALU.mult).then_inc(misc_done, 1)
                    nc.vector.tensor_tensor(r[:, 0, 0, :], bank[6], cosT, ALU.mult)
                    nc.vector.tensor_tensor(r[:, 1, 1, :], bank[6], sinT, ALU.mult).then_inc(rot_m, 1)
                elif kind == "ks":
                    i = item[1]
                    dve.wait_ge(kh_sb, i + 1)
                    rounded, rest = key_parts(i)
                    nc.vector.tensor_tensor(rest, rest, rounded, ALU.subtract).then_inc(kl_sb, 1)
                elif kind == "q1":
                    n = item[1]
                    dve.wait_ge(qh_sb, n + 1)
                    nc.vector.tensor_tensor(qq[n % 2][:, 1, :], bank[6], qq[n % 2][:, 0, :].bitcast(f32),
                                            ALU.subtract).then_inc(ql_sb, 1)
                elif kind == "ln1":
                    _, b, i = item
                    if i:
                        norm_apply(y, x if i == 1 else y, b * QT, QT)
                    if i == 1:
                        dve.wait_ge(normed, norm[item])
                    if i < 2:
                        norm_stats(y if i else x, b * QT, QT)
                elif kind == "s1":
                    u = item[1]
                    dve.wait_ge(st_exp, UNITS + u + 1)
                    nc.vector.tensor_scalar(prob[:, u % RING1, :], prob[:, u % RING1, :], math.exp(-CLIP),
                                            math.exp(CLIP), ALU.max, ALU.min).then_inc(clipped, 1)
                elif kind == "o1":
                    n = item[1]
                    dve.wait_ge(pv1, n + 1)
                    link(nc.vector.reciprocal(rs1[:, n % 2, :], bank[4 + n % 2][:, S:2 * S]))
                    nc.vector.tensor_tensor(oT1[:, n // PAIRS, n % PAIRS, :],
                                            bank[4 + n % 2][:, 0:S], rs1[:, n % 2, :], ALU.mult).then_inc(o1_sb, 1)
                    if n == 3:
                        nc.vector.tensor_reduce(sc[:, 1:2], wf[:, :], AX.X, ALU.add,
                                                apply_absolute_value=True).then_inc(sc_sb, 1)
                    elif n == UNITS // 2 - 1:
                        nc.vector.tensor_scalar_mul(sc[:, 4:5], sc[:, 2:3], 0.5)
                        link(nc.vector.tensor_scalar_mul(sc[:, 5:6], sc[:, 2:3], -0.5))
                        link(nc.vector.tensor_scalar(qw[:, 1, :], wf[:, :], sc[:, 5:6], None, ALU.is_lt))
                        link(nc.vector.scalar_tensor_tensor(out=qw[:, 0, :], in0=wf[:, :], scalar=sc[:, 4:5],
                                                            in1=qw[:, 1, :], op0=ALU.is_gt, op1=ALU.subtract))

            dve.wait_ge(sc_ps, 1)
            link(nc.vector.tensor_reduce(sc[:, 1:2], bank[7][:, 0:2 * P], AX.X, ALU.max))
            link(nc.vector.tensor_scalar_mul(sc[:, 5:6], sc[:, 1:2], 1.0 / 127.0))
            link(nc.vector.reciprocal(sc[:, 6:7], sc[:, 5:6]))
            link(nc.vector.tensor_scalar(qz[:, :, :], y[:, :, :], sc[:, 6:7], MAGIC, ALU.mult, ALU.add))
            nc.vector.tensor_scalar(qzb[:, :, :], qz[:, :, :], MAGIC, -128.0, ALU.subtract, ALU.max).then_inc(qz_sb, 1)
            link(nc.vector.tensor_tensor(sc[:, 7:8], sc[:, 5:6], sc[:, 2:3], ALU.mult))
            dve.wait_ge(qz_ps, 1)
            nc.vector.tensor_scalar(qzT[:, :], bank[4].bitcast(bf16)[:, 0:T], 127.0, None, ALU.min).then_inc(qzT_sb, 1)
            dve.wait_ge(xbias, 1 + 2 * B)
            dve.wait_ge(f_ps, 1)
            nc.vector.scalar_tensor_tensor(out=qz[:, :, :], in0=bank[6].rearrange("p (t d) -> p t d", t=TT),
                                           scalar=sc[:, 7:8], in1=xb[:, :, :], op0=ALU.mult, op1=ALU.add).then_inc(fin, 1)

        @block.tensor
        def _(pe):
            def mm(o, l, r, start=True, stop=True):
                return nc.tensor.matmul(o, l, r, start=start, stop=stop)

            def transposes(src, first, tiles, dst):
                for t in range(tiles):
                    last = nc.tensor.transpose(dst[:, t * P:(t + 1) * P], src[:, first + t, :], ident[:, :])
                return last

            def values(n):
                if n >= 4:
                    pe.wait_ge(v1_sb, n - 3)
                mm(bank[n % 4], ctxT[:, (n // 2) * P:(n // 2 + 1) * P],
                   wv1[:, 512 * (n % 2):512 * (n % 2) + 512]).then_inc(v1_ps, 1)

            def free(item):
                if misc[item] > 1:
                    pe.wait_ge(misc_done, misc[item] - 1)

            pe.wait_ge(in_w0, 16)
            pe.wait_ge(in_ctxT, 16)
            mm(bank[4], l0w[:, 1, :], ctxT[:, 0:S2]).then_inc(k0_ps, 1)
            pe.wait_ge(consts, 1)
            pe.wait_ge(normed, 1)
            transposes(y, 0, TT, bank[7]).then_inc(tr, 1)
            mm(bank[5], l0w[:, 1, :], ctxT[:, S2:2 * S2]).then_inc(k0_ps, 1)
            pe.wait_ge(yT_sb, 1)
            mm(bank[6], l0w[:, 0, :], yT[:, :]).then_inc(q0_ps, 1)
            for i in range(2):
                for c in range(4):
                    ct = 4 * i + c
                    last = mm(bank[2 + i][:, c * D:(c + 1) * D], ctxT[:, ct * P:(ct + 1) * P], l0w[:, 2, :])
                last.then_inc(v0_ps, 1)
            pe.wait_ge(ctx_normed, 1)
            for i in range(2):
                transposes(ctx_tok, 4 * i, 4, bank[i]).then_inc(tr, 1)
            pe.wait_ge(in_wv, 16)
            pe.wait_ge(v0_sb, 2)
            pe.wait_ge(ctxn, 2)
            for n in range(EARLY):
                values(n)

            mx = 0
            for item in order:
                kind = item[0]
                if item in misc:
                    free(item)
                if kind == "v1":
                    values(item[1])
                elif kind == "mx":
                    _, q, i = item
                    b, h, t = q // 2, 8 * (q % 2) + i // 2, i % 2
                    if q % 2 == 0 and i == 0:
                        if b == 0:
                            pe.wait_ge(parts, 3)
                        pe.wait_ge(stack[b], 16 * 8)
                    mx += 1
                    if mx > 2:
                        pe.wait_ge(mx_done, mx - 2)
                    mm(bank[4 + mx % 2], Qs[0:MAX_ROW, b, h, t * P:(t + 1) * P], Ks[0:MAX_ROW, b, h, :]).then_inc(mx_ps, 1)
                elif kind == "mt":
                    q = item[1]
                    pe.wait_ge(mx_done, (q + 1) * H)
                    nc.tensor.transpose(bank[7][0:H, 0:P], nmax[:, q, :],
                                        ident[:, :]).then_inc(misc_ps, 1)
                elif kind == "st":
                    u = item[1]
                    b, h = u // H, u % H
                    if u % 8 == 0:
                        pe.wait_ge(max_rows[u // 8], 16 * NPART)
                    if u == 0:
                        pe.wait_ge(v1_sb, 2 * CT)
                    if u >= 2:
                        pe.wait_ge(st_exp, u - 1)
                    for k in range(KT):
                        last = mm(st2[u % 2][:, k * S:(k + 1) * S], Ks[:, b, h, k * P:(k + 1) * P], Qs[:, b, h, :])
                    last.then_inc(st_ps, 1)
                elif kind == "pv":
                    _, g, k = item
                    b = g // G
                    if k == 0:
                        pe.wait_ge(st_exp, 4 * g + 4)
                        pe.wait_ge(o0_sb, g + 1)
                    for j in range(4):
                        u = 4 * g + j
                        last = mm(bank[6][32 * j:32 * j + DK0 + 1, 0:S], v0[:, b * KT + k, u % H, :],
                                  prob[:, u % RING, k * S:(k + 1) * S], start=(k == 0), stop=(k == KT - 1))
                    if k == KT - 1:
                        last.then_inc(pv0, 1)
                elif kind == "t1":
                    t = item[1]
                    b, half = t // QT, t % QT
                    pe.wait_ge(o0_sb, G * (b + 1) + 1)
                    for g in range(G):
                        last = nc.tensor.transpose(bank[7][:, g * P:(g + 1) * P],
                                                   o0[:, b * G + g, half * P:(half + 1) * P], ident[:, :])
                    last.then_inc(misc_ps, 1)
                elif kind == "t2":
                    b = item[1]
                    for t in range(QT):
                        last = nc.tensor.transpose(bank[7][:, t * P:(t + 1) * P],
                                                   on0[:, b * QT + t, :, :].rearrange("p h d -> p (h d)"), ident[:, :])
                    last.then_inc(misc_ps, 1)
                elif kind == "wo":
                    b = item[1]
                    for t in range(QT):
                        last = mm(bank[7][:, t * D:(t + 1) * D], oT0[:, (b * QT + t) * P:(b * QT + t + 1) * P], l0w[:, 3, :])
                    last.then_inc(misc_ps, 1)
                elif kind in ("yt", "l1t"):
                    b = item[1]
                    pe.wait_ge(normed, norm[("wo", b) if kind == "yt" else ("ln1", b, 2)])
                    transposes(y, b * QT, QT, bank[7]).then_inc(misc_ps, 1)
                elif kind == "rt":
                    b = item[1]
                    pe.wait_ge(in_small, 16 * 8)
                    for t in range(QT):
                        last = mm(bank[7][:, t * E:(t + 1) * E], yT[:, (b * QT + t) * P:(b * QT + t + 1) * P], wr[:, :])
                    last.then_inc(misc_ps, 1)
                elif kind == "wt":
                    b = item[1]
                    pe.wait_ge(rt_w, b + 1)
                    for t in range(QT):
                        last = nc.tensor.transpose(bank[7][0:E, t * P:(t + 1) * P], wgt[:, b * QT + t, :], ident[:, :])
                    last.then_inc(misc_ps, 1)
                elif kind == "b2":
                    b = item[1]
                    for t in range(QT):
                        last = mm(bank[7][:, t * D:(t + 1) * D], wT[:, (b * QT + t) * P:(b * QT + t + 1) * P], b2[:, :])
                    last.then_inc(misc_ps, 1)
                elif kind == "hid":
                    n = item[1]
                    b, e = n // E, n % E
                    if n == 0:
                        pe.wait_ge(st_exp, UNITS)
                        pe.wait_ge(in_w1, 16)
                    if n % E == 0:
                        pe.wait_ge(misc_done, misc[("yt", b)])
                    for f in range(FT):
                        if n >= 1:
                            pe.wait_ge(h_sb, (n - 1) * FT + f + 1)
                        mm(bank[f][:, 0:S], w1[:, e, f * P:(f + 1) * P], yT[:, b * S:(b + 1) * S]).then_inc(h_ps, 1)
                elif kind == "yy":
                    n = item[1]
                    b, e = n // E, n % E
                    if n == 0:
                        pe.wait_ge(in_w2, 16)
                        pe.wait_ge(mx_done, UNITS * QT)
                    if n >= 2:
                        pe.wait_ge(y_acc, n - 1)
                    pe.wait_ge(h_sb, FT * (n + 1))
                    for t in range(QT):
                        for f in range(FT):
                            last = mm(bank[4 + n % 2][:, t * D:(t + 1) * D], hT[:, n % 2, f, t * P:(t + 1) * P],
                                      w2[:, e, f, :], start=(f == 0), stop=(f == FT - 1))
                    last.then_inc(y_ps, 1)
                elif kind == "kp":
                    n = item[1]
                    b, g = n // G, n % G
                    if n == 0:
                        pe.wait_ge(in_wk, 16)
                        pe.wait_ge(o0_sb, B * G + 1)
                    else:
                        pe.wait_ge(rot_m, n)
                    for part in range(2):
                        last = mm(bank[6 + part], wk1[:, 2 * g + part, :], ctxT[:, b * S2:(b + 1) * S2])
                    last.then_inc(misc_ps, 1)
                elif kind == "q1":
                    n = item[1]
                    b, p = n // PAIRS, n % PAIRS
                    if p == 0:
                        pe.wait_ge(misc_done, misc[("l1t", b)])
                        pe.wait_ge(in_wq, 16)
                    if n:
                        pe.wait_ge(ql_sb, n)
                    else:
                        pe.wait_ge(rot_m, B * G)
                    for e in range(2):
                        for twice in range(2):
                            w = (2 * p + e) * DK1
                            last = mm(bank[6][twice * DK1:(twice + 1) * DK1, e * S:(e + 1) * S], wq1[:, w:w + DK1],
                                      yT[:, b * S:(b + 1) * S])
                    last.then_inc(q1_ps, 1)
                elif kind == "s1":
                    u = item[1]
                    b, h = u // H, u % H
                    if u % 2 == 0:
                        pe.wait_ge(ql_sb, u // 2 + 1)
                    if u == 0:
                        pe.wait_ge(h_sb, B * E * FT)
                    if h == 0:
                        for i in range(2):
                            pe.wait_ge(kst_out[b][i], 16 * 16)
                    if u >= 2:
                        pe.wait_ge(st_exp, UNITS + u - 1)
                    for k in range(KT):
                        for part in range(2):
                            last = mm(st2[u % 2][:, k * S:(k + 1) * S], stacked(b, h)[:, k * P:(k + 1) * P],
                                      qq[u // 2 % 2][:, part, (h % 2) * S:(h % 2 + 1) * S], start=(part == 0), stop=(part == 1))
                    last.then_inc(st_ps, 1)
                elif kind == "o1":
                    n = item[1]
                    b, p = n // PAIRS, n % PAIRS
                    pe.wait_ge(clipped, 2 * n + 2)
                    if n >= 2:
                        pe.wait_ge(o1_sb, n - 1)
                    elif n == 0:
                        pe.wait_ge(y_acc, B * E)
                    dst = bank[4 + n % 2]
                    for k in range(KT):
                        for e in range(2):
                            h = 2 * p + e
                            mm(dst[64 * e:64 * e + 64, 0:S], v1[:, b * KT + k, h * DK1:(h + 1) * DK1],
                               prob[:, (2 * n + e) % RING1, k * S:(k + 1) * S], start=(k == 0), stop=(k == KT - 1))
                    pe.wait_ge(summed, 2 * n + 2)
                    for e in range(2):
                        last = mm(dst[64 * e:64 * e + 64, S:2 * S], ones[:, 0:64], sums[:, (2 * n + e) % 4, :])
                    last.then_inc(pv1, 1)
                elif kind == "w1p":
                    pe.wait_ge(misc_done, misc[("w1o", 1)] - 1)
                    pe.wait_ge(ql_sb, UNITS // 2)
                    pe.wait_ge(o1_sb, PAIRS + item[2])
                    for t in range(QT):
                        for p in range(item[1], item[2]):
                            mm(bank[7 - t][:, 0:D], oT1[:, 1, p, t * P:(t + 1) * P], wo1[:, p, :],
                               start=(p == 0), stop=False)
                elif kind == "w1o":
                    b = item[1]
                    if b == 0:
                        pe.wait_ge(in_wo, 16)
                        pe.wait_ge(sc_sb, 1)
                        mm(bank[7][:, S:S + 1], ones[:, :], sc[:, 1:2])
                    pe.wait_ge(o1_sb, PAIRS * (b + 1))
                    for t in range(QT):
                        if b == 1:
                            p = PAIRS - 1
                            last = mm(bank[7 - t][:, 0:D], oT1[:, b, p, t * P:(t + 1) * P], wo1[:, p, :], start=False)
                            continue
                        for p in range(PAIRS):
                            last = mm(bank[7][:, t * D:(t + 1) * D], oT1[:, b, p, t * P:(t + 1) * P], wo1[:, p, :],
                                      start=(p == 0), stop=(p == PAIRS - 1))
                    last.then_inc(misc_ps, 1)

            pe.wait_ge(misc_done, len(misc))
            for b in range(B):
                pe.wait_ge(sc_sb, 2 + b)
                last = mm(bank[7][:, b * P:(b + 1) * P], sc[:, 3 * b:3 * b + 1].broadcast_to([P, P]), ident[:, :])
            last.then_inc(sc_ps, 1)
            pe.wait_ge(qz_sb, 1)
            for t in range(TT):
                last = nc.tensor.transpose(bank[4].bitcast(bf16)[:, t * P:(t + 1) * P], qzb[:, t, :], identb[:, :])
            last.then_inc(qz_ps, 1)
            pe.wait_ge(qzT_sb, 1)
            for t in range(TT):
                last = mm(bank[6][:, t * D:(t + 1) * D], qzT[:, t * P:(t + 1) * P], qw[:, 0, :])
            last.then_inc(f_ps, 1)


def kernel(**inputs):
    import concourse.bacc as bacc
    from concourse.bass_utils import run_bass_kernel_spmd

    v = {n: np.asarray(a) for n, a in inputs.items()}
    dh = np.arange(D).reshape(H, DK0).T.reshape(-1)
    wkv = v["L1_xattn_Wkv"]
    wk = wkv[:, :H * DK1].reshape(D, G, 4, 2, 32).transpose(0, 1, 3, 2, 4).reshape(D, H * DK1)
    arrays = {
        "x": v["x"].reshape(TT, P, D),
        "ctx": v["ctx_1024"].reshape(CT, P, D),
        "ctxT": v["ctx_1024"].reshape(C, D).T,
        "mask": v["mask_BxS2_bf1"].reshape(1, C).view(np.uint8),
        "l0w": np.stack([v["L0_xattn_Wq"].T[:, dh], v["L0_xattn_Wk"].T[:, dh], v["L0_xattn_Wv"].T, v["L0_xattn_Wo"].T]),
        "bias0": v["L0_xattn_bo"].reshape(1, D),
        "bias1": v["L1_xattn_bo"].reshape(1, D),
        "bias2": v["L1_ffn_bias"].reshape(1, D),
        "brow": v["L0_ffn_b_router"].reshape(1, E),
        "lncol": np.stack([v["L1_xattn_ln_" + n] for n in ("lat_g", "lat_b", "ctx_g", "ctx_b")], axis=1),
        "wr": v["L0_ffn_W_router"], "w1": v["L0_ffn_W1"], "w2": v["L0_ffn_W2"],
        "b1": v["L0_ffn_b1"].reshape(E, FT, P).transpose(2, 0, 1), "b2": v["L0_ffn_b2"],
        "cosT": v["L1_xattn_cos"].T, "sinT": v["L1_xattn_sin"].T,
        "wq1": v["L1_xattn_Wq"], "wk1": wk, "wv1": wkv[:, H * DK1:], "wo1": v["L1_xattn_Wo"],
        "wf": v["L1_ffn_weight"].T,
    }
    arrays = {n: np.ascontiguousarray(a) for n, a in arrays.items()}
    nc = bacc.Bacc("TRN2", target_bir_lowering=False, num_devices=1)
    aps = {n: nc.dram_tensor("in_" + n, a.shape, mybir.dt.from_np(a.dtype), kind="ExternalInput").ap()
           for n, a in arrays.items()}
    out = nc.dram_tensor("out_0", (TT, P, D), mybir.dt.float32, kind="ExternalOutput").ap()
    build(nc, aps, out)
    r = run_bass_kernel_spmd(nc, [{"in_" + n: a for n, a in arrays.items()}], core_ids=[0])
    return r.results[0]["out_0"].reshape(B, S, D)
```
